# Optimizing a Trainium2 kernel written in Bass

```python
import numpy as np
import jax
import jax.numpy as jnp

def _softmax(x, axis=-1):
    return jax.nn.softmax(x, axis=axis)

def _gelu(x):
    return jax.nn.gelu(x, approximate=True)

def _silu(x):
    return jax.nn.silu(x)

def _sigmoid(x):
    return jax.nn.sigmoid(x)

def _layernorm(x, axis=-1, eps=1e-05):
    m = jnp.mean(x, axis=axis, keepdims=True)
    v = jnp.var(x, axis=axis, keepdims=True)
    return (x - m) / jnp.sqrt(v + eps)

def _scatter_add(tgt, idx, src, axis=0):
    return tgt.at[idx].add(src)

def _segment_sum(src, seg, n):
    return jax.ops.segment_sum(src, seg, n)
kernel_name = 'mk_cond_resid_d4_seqx_r4_e9dcd7'

def setup_inputs(seed: int=0):
    np.random.seed(seed)
    _w = jnp.asarray

    def _rec_inputs():
        import jax
        import jax.numpy as jnp
        _rk = jax.random.key(seed)
        x = -0.0003929 + 0.9999 * jax.random.normal(jax.random.fold_in(_rk, 1), (128, 64, 256), jnp.float32)
        _lenS = 64 - jax.random.randint(jax.random.fold_in(_rk, 7), (128,), 0, max(1, 64 // 4) + 1, jnp.int32)
        _lenS2 = 64 - jax.random.randint(jax.random.fold_in(_rk, 8), (128,), 0, max(1, 64 // 4) + 1, jnp.int32)
        itok_B_0_7 = jax.random.randint(jax.random.fold_in(_rk, 11), (128,), 0, 8, jnp.int32)
        condB_deltat = jax.random.uniform(jax.random.fold_in(_rk, 12), (128,), jnp.float32, 0.0, 1.99976)
        itok_B_0_63 = jax.random.randint(jax.random.fold_in(_rk, 13), (128,), 0, 64, jnp.int32)
        return (x, itok_B_0_7, condB_deltat, itok_B_0_63)
    x, itok_B_0_7, condB_deltat, itok_B_0_63 = _rec_inputs()

    def _L0_cond_setup():
        import jax, jax.numpy as jnp
        import numpy as np
        S, O, H = (8, 256, 256)
        B, N = (32, 128)
        key = jax.random.key(seed)
        k1, k2, k3, k4 = jax.random.split(key, 4)
        x = jax.random.normal(k1, (B, N, H), dtype=jnp.float32)
        subject_id = jax.random.randint(k2, (B,), 0, S)
        wbound = jnp.sqrt(2.0 / 6.0) * jnp.sqrt(3.0 / H)
        weight = jax.random.uniform(k3, (S, O, H), minval=-wbound, maxval=wbound, dtype=jnp.float32)
        bbound = 1.0 / jnp.sqrt(H)
        bias = jax.random.uniform(k4, (S, O), minval=-bbound, maxval=bbound, dtype=jnp.float32)
        return {'x': x, 'subject_id': subject_id, 'weight': weight, 'bias': bias}
    _L0_cond_all = _L0_cond_setup()
    _L0_cond_in = {k: v for k, v in _L0_cond_all.items() if k in ('weight', 'bias')}
    del _L0_cond_all

    def _L1_cond_setup():
        import jax, jax.numpy as jnp
        import numpy as np
        B, F, T = (64, 64, 256)
        key = jax.random.key(seed)
        k1, k2, k3, k4 = jax.random.split(key, 4)
        x = jax.random.normal(k1, (B, 2 * F, T), dtype=jnp.float32)
        delta_t = jax.random.uniform(k2, (B,), dtype=jnp.float32, minval=0.5, maxval=2.0)
        amplitudes = jax.random.uniform(k3, (F,), dtype=jnp.float32, minval=0.7, maxval=1.3)
        frequencies = jax.random.uniform(k4, (F,), dtype=jnp.float32, minval=0.0, maxval=2.0 * np.pi)
        return {'x': x, 'delta_t': delta_t, 'amplitudes': amplitudes, 'frequencies': frequencies}
    _L1_cond_all = _L1_cond_setup()
    _L1_cond_in = {k: v for k, v in _L1_cond_all.items() if k in ('amplitudes', 'frequencies')}
    del _L1_cond_all

    def _L2_cond_setup():
        import jax, jax.numpy as jnp
        import numpy as np
        NUM_CATEGORIES = 64
        INPUT_DIM = 256
        HIDDEN_DIM = 256
        B = 64
        S = 64
        key = jax.random.key(seed)
        kx, kc, kw = jax.random.split(key, 3)
        x = jax.random.normal(kx, (B, S, INPUT_DIM), dtype=jnp.float32)
        cat_ids = jax.random.randint(kc, (B,), 0, NUM_CATEGORIES, dtype=jnp.int32)
        W = 0.02 * jax.random.normal(kw, (NUM_CATEGORIES, INPUT_DIM, HIDDEN_DIM), dtype=jnp.float32)
        b = jnp.zeros((NUM_CATEGORIES, HIDDEN_DIM), dtype=jnp.float32)
        return {'x': x, 'cat_ids': cat_ids, 'W': W, 'b': b}
    _L2_cond_all = _L2_cond_setup()
    _L2_cond_in = {k: v for k, v in _L2_cond_all.items() if k in ('W', 'b')}
    del _L2_cond_all

    def _L3_cond_setup():
        import jax, jax.numpy as jnp
        import numpy as np
        B, S, D, F = (32, 128, 256, 1024)
        R_COMMON, R_DOMAIN, E = (16, 16, 8)
        ALPHA = 2.0

        def _expert_lora(x, expert_ids, Wa, Wb):
            Ab = Wa[expert_ids]
            Bb = Wb[expert_ids]
            low = jnp.einsum('bsd,brd->bsr', x, Ab)
            return ALPHA * jnp.einsum('bsr,bor->bso', low, Bb)
        key = jax.random.key(seed)
        ks = jax.random.split(key, 12)
        sd = lambda k, shape: jax.random.normal(k, shape, dtype=jnp.float32) * (1.0 / np.sqrt(shape[-1]))
        return {'hidden_states': jax.random.normal(ks[0], (B, S, D), dtype=jnp.float32), 'expert_ids': jax.random.randint(ks[1], (B,), 0, E, dtype=jnp.int32), 'wi': sd(ks[2], (F, D)), 'wo': sd(ks[3], (D, F)), 'common_wi_a': sd(ks[4], (R_COMMON, D)), 'common_wi_b': sd(ks[5], (F, R_COMMON)), 'common_wo_a': sd(ks[6], (R_COMMON, F)), 'common_wo_b': sd(ks[7], (D, R_COMMON)), 'experts_wi_a': sd(ks[8], (E, R_DOMAIN, D)), 'experts_wi_b': sd(ks[9], (F, R_DOMAIN)) * jnp.ones((E, 1, 1)) * 0.0 + sd(ks[9], (E, F, R_DOMAIN)), 'experts_wo_a': sd(ks[10], (E, R_DOMAIN, F)), 'experts_wo_b': sd(ks[11], (E, D, R_DOMAIN))}
    _L3_cond_all = _L3_cond_setup()
    _L3_cond_in = {k: v for k, v in _L3_cond_all.items() if k in ('wi', 'wo', 'common_wi_a', 'common_wi_b', 'common_wo_a', 'common_wo_b', 'experts_wi_a', 'experts_wi_b', 'experts_wo_a', 'experts_wo_b')}
    del _L3_cond_all
    return {'x': x, 'itok_B_0_7': itok_B_0_7, 'condB_deltat': condB_deltat, 'itok_B_0_63': itok_B_0_63, 'L0_cond_weight': _L0_cond_in['weight'], 'L0_cond_bias': _L0_cond_in['bias'], 'L1_cond_amplitudes': _L1_cond_in['amplitudes'], 'L1_cond_frequencies': _L1_cond_in['frequencies'], 'L2_cond_W': _L2_cond_in['W'], 'L2_cond_b': _L2_cond_in['b'], 'L3_cond_wi': _L3_cond_in['wi'], 'L3_cond_wo': _L3_cond_in['wo'], 'L3_cond_common_wi_a': _L3_cond_in['common_wi_a'], 'L3_cond_common_wi_b': _L3_cond_in['common_wi_b'], 'L3_cond_common_wo_a': _L3_cond_in['common_wo_a'], 'L3_cond_common_wo_b': _L3_cond_in['common_wo_b'], 'L3_cond_experts_wi_a': _L3_cond_in['experts_wi_a'], 'L3_cond_experts_wi_b': _L3_cond_in['experts_wi_b'], 'L3_cond_experts_wo_a': _L3_cond_in['experts_wo_a'], 'L3_cond_experts_wo_b': _L3_cond_in['experts_wo_b']}

def reference(x, itok_B_0_7, condB_deltat, itok_B_0_63, L0_cond_weight, L0_cond_bias, L1_cond_amplitudes, L1_cond_frequencies, L2_cond_W, L2_cond_b, L3_cond_wi, L3_cond_wo, L3_cond_common_wi_a, L3_cond_common_wi_b, L3_cond_common_wo_a, L3_cond_common_wo_b, L3_cond_experts_wi_a, L3_cond_experts_wi_b, L3_cond_experts_wo_a, L3_cond_experts_wo_b):
    import jax
    import jax.numpy as jnp

    def _L0_cond_ref(x, subject_id, weight, bias):
        import jax, jax.numpy as jnp
        import numpy as np
        S, O, H = (8, 256, 256)
        B, N = (32, 128)
        W = weight[subject_id]
        b = bias[subject_id]
        y = jnp.einsum('bnh,boh->bno', x, W) + b[:, None, :]
        return y

    def _L1_cond_ref(x, delta_t, amplitudes, frequencies):
        import jax, jax.numpy as jnp
        import numpy as np
        B, F, T = (64, 64, 256)
        Bn = x.shape[0]
        Fn = amplitudes.shape[0]
        a = amplitudes[None, :] ** delta_t[:, None]
        ang = frequencies[None, :] * delta_t[:, None]
        c = a * jnp.cos(ang)
        s = a * jnp.sin(ang)
        xr = x.reshape(Bn, Fn, 2, -1)
        x0, x1 = (xr[:, :, 0], xr[:, :, 1])
        out0 = c[..., None] * x0 - s[..., None] * x1
        out1 = s[..., None] * x0 + c[..., None] * x1
        return jnp.stack([out0, out1], axis=2).reshape(x.shape)

    def _L2_cond_ref(x, cat_ids, W, b):
        import jax, jax.numpy as jnp
        import numpy as np
        NUM_CATEGORIES = 64
        INPUT_DIM = 256
        HIDDEN_DIM = 256
        B = 64
        S = 64
        selected_W = W[cat_ids]
        selected_b = b[cat_ids]
        out = jnp.einsum('bsd,bdh->bsh', x, selected_W) + selected_b[:, None, :]
        return out

    def _L3_cond_ref(hidden_states, expert_ids, wi, wo, common_wi_a, common_wi_b, common_wo_a, common_wo_b, experts_wi_a, experts_wi_b, experts_wo_a, experts_wo_b):
        import jax, jax.numpy as jnp
        import numpy as np
        B, S, D, F = (32, 128, 256, 1024)
        R_COMMON, R_DOMAIN, E = (16, 16, 8)
        ALPHA = 2.0

        def _expert_lora(x, expert_ids, Wa, Wb):
            Ab = Wa[expert_ids]
            Bb = Wb[expert_ids]
            low = jnp.einsum('bsd,brd->bsr', x, Ab)
            return ALPHA * jnp.einsum('bsr,bor->bso', low, Bb)
        x = hidden_states
        hidden_i = jnp.einsum('bsd,fd->bsf', x, wi)
        hidden_i += ALPHA * jnp.einsum('bsr,fr->bsf', jnp.einsum('bsd,rd->bsr', x, common_wi_a), common_wi_b)
        hidden_i += _expert_lora(x, expert_ids, experts_wi_a, experts_wi_b)
        hidden_i = jax.nn.relu(hidden_i)
        hidden_o = jnp.einsum('bsf,df->bsd', hidden_i, wo)
        hidden_o += ALPHA * jnp.einsum('bsr,dr->bsd', jnp.einsum('bsf,rf->bsr', hidden_i, common_wo_a), common_wo_b)
        hidden_o += _expert_lora(hidden_i, expert_ids, experts_wo_a, experts_wo_b)
        return hidden_o
    x = x + _L0_cond_ref(x, itok_B_0_7, L0_cond_weight, L0_cond_bias)
    x = x + _L1_cond_ref(x, condB_deltat, L1_cond_amplitudes, L1_cond_frequencies)
    x = x + _L2_cond_ref(x, itok_B_0_63, L2_cond_W, L2_cond_b)
    x = x + _L3_cond_ref(x, itok_B_0_7, L3_cond_wi, L3_cond_wo, L3_cond_common_wi_a, L3_cond_common_wi_b, L3_cond_common_wo_a, L3_cond_common_wo_b, L3_cond_experts_wi_a, L3_cond_experts_wi_b, L3_cond_experts_wo_a, L3_cond_experts_wo_b)
    return x

_drawn_inputs = setup_inputs


def setup_inputs(seed=0):
    import zlib

    import numpy as np

    out = dict(_drawn_inputs(seed))
    spreads = {'L2_cond_b': (0.0, 0.1)}
    factors = {}
    for name, (base, spread) in spreads.items():
        noise = np.random.default_rng([zlib.crc32(name.encode()), seed]).standard_normal(out[name].shape)
        drawn = base * np.exp(spread * noise) if base else spread * noise
        out[name] = jnp.asarray(drawn.astype(out[name].dtype))
    for name, factor in factors.items():
        out[name] = (out[name] * factor).astype(out[name].dtype)
    return out
```

```python
from contextlib import ExitStack

import numpy as np

import concourse.bass as bass
from concourse import mybir

FP32 = mybir.dt.float32
F32R = mybir.dt.float32r
BF16 = mybir.dt.bfloat16
I32 = mybir.dt.int32
ALU = mybir.AluOpType
ACT = mybir.ActivationFunctionType

P = 128
BATCH, SEQ, D = 128, 64, 256
F = 1024
EXPERTS, RANK = 8, 16
CATEGORIES = 64
SPG = 4
GT = SPG * SEQ
GROUPS = BATCH // SPG
TILES = GT // P
HALVES = D // P
FT = F // P
PAIRS = FT // 2
PARTS = 3
PRODUCTS = [(2, 0), (0, 2), (1, 1), (1, 0), (0, 1), (0, 0)]
ALPHA = 2.0


def stack_constants():
    place = np.zeros((P, 2, PARTS, P), np.float32)
    for q, (w_part, a_part) in enumerate(PRODUCTS):
        for r in range(RANK):
            place[r::RANK, 0, a_part, RANK * q + r] = 1.0
            place[r::RANK, 1, w_part, RANK * q + r] = 1.0
    return place.reshape(P, 2, PARTS * P)


def small_constants():
    small = np.zeros((P, 1 + EXPERTS), np.float32)
    small[:, 0] = np.arange(P)
    for e in range(EXPERTS):
        small[RANK * e:RANK * (e + 1), 1 + e] = 1.0
    return small


def cond_resid_kernel(nc, x, experts, delta_t, cats, w0, b0, amplitudes, frequencies, w2, b2, wi, wo,
                      common_wi_a, common_wi_b, common_wo_a, common_wo_b,
                      experts_wi_a, experts_wi_b, experts_wo_a, experts_wo_b,
                      identity, place, small, out):
    x_rows = x.rearrange("b s d -> (b s) d").rearrange("(q t p) d -> q p t d", t=TILES, p=P)
    out_rows = out.rearrange("b s d -> (b s) d").rearrange("(q t p) d -> q p t d", t=TILES, p=P)
    rotation_dram = nc.dram_tensor("rotation_scratch", (2, BATCH * SEQ), FP32, kind="Internal").ap()

    ctx = ExitStack()
    with ctx:
        def sb(name, shape, dtype=FP32, stack=ctx):
            return stack.enter_context(nc.sbuf_tensor(name, shape, dtype))

        def sem(name):
            return ctx.enter_context(nc.semaphore(name))

        ident = sb("ident", [P, P])
        small_sb = sb("small_sb", [P, 1 + EXPERTS])
        wi_hi, wi_lo = (sb(f"wi_{n}", [P, HALVES, F], F32R) for n in ("hi", "lo"))
        wo_hi, wo_lo = (sb(f"wo_{n}", [P, FT, D], F32R) for n in ("hi", "lo"))
        ia_hi, ia_lo = (sb(f"ia_{n}", [P, HALVES, P], F32R) for n in ("hi", "lo"))
        oa_hi, oa_lo = (sb(f"oa_{n}", [P, FT, P], F32R) for n in ("hi", "lo"))
        w0_parts = sb("w0_parts", [P, EXPERTS, PARTS, HALVES * D], BF16)
        ib_stack = sb("ib_stack", [P, EXPERTS, F], BF16)
        ob_stack = sb("ob_stack", [P, EXPERTS, D], BF16)
        pick = sb("pick", [P, EXPERTS, PARTS * P], BF16)
        bias = sb("bias", [P, 2 * HALVES, BATCH])
        index = sb("index", [1, 2, BATCH], I32)

        x_sb = sb("x_sb", [P, TILES, D])
        rotation = sb("rotation", [P, 2, GT])
        w2_raw = sb("w2_raw", [P, SPG, HALVES * D])
        hid_hi, hid_lo = (sb(f"hid_{n}", [P, FT, GT], F32R) for n in ("hi", "lo"))
        y2_hi, y2_lo = (sb(f"y2_{n}", [P, HALVES, GT], F32R) for n in ("hi", "lo"))
        out_sb = sb("out_sb", [P, TILES, D])

        scratch = ExitStack()
        wi_nat = sb("wi_nat", [P, FT, D], FP32, scratch)
        wo_nat = sb("wo_nat", [P, HALVES, F], FP32, scratch)
        w0_nat = sb("w0_nat", [P, 2, HALVES, D], FP32, scratch)
        ia_nat = sb("ia_nat", [P, D], FP32, scratch)
        ib_nat = sb("ib_nat", [P, FT, P], FP32, scratch)
        oa_nat = sb("oa_nat", [P, F], FP32, scratch)
        ob_nat = sb("ob_nat", [P, HALVES, P], FP32, scratch)
        cia = sb("cia", [RANK, D], FP32, scratch)
        cib_nat = sb("cib_nat", [P, FT, RANK], FP32, scratch)
        coa = sb("coa", [RANK, F], FP32, scratch)
        cob_nat = sb("cob_nat", [P, HALVES, RANK], FP32, scratch)
        cia2 = sb("cia2", [RANK, D], FP32, scratch)
        coa2 = sb("coa2", [RANK, F], FP32, scratch)
        cib_t = sb("cib_t", [RANK, F], FP32, scratch)
        cob_t = sb("cob_t", [RANK, D], FP32, scratch)
        place_sb = sb("place_sb", [P, 2, PARTS * P], FP32, scratch)
        put = sb("put", [P, EXPERTS, PARTS * P], BF16, scratch)
        ib_parts = sb("ib_parts", [P, PARTS, F], BF16, scratch)
        ob_parts = sb("ob_parts", [P, PARTS, D], BF16, scratch)
        rest = sb("rest", [P, 2, 512], FP32, scratch)
        b0_nat = sb("b0_nat", [EXPERTS, D], FP32, scratch)
        b2_nat = sb("b2_nat", [CATEGORIES, D], FP32, scratch)
        index_all = sb("index_all", [CATEGORIES, 2, BATCH], I32, scratch)
        index_f = sb("index_f", [CATEGORIES, 2, BATCH], FP32, scratch)
        one_hot = sb("one_hot", [CATEGORIES, 2, BATCH], FP32, scratch)
        rot = sb("rot", [P, 14, SEQ], FP32, scratch)
        dt_sb = sb("dt_sb", [P, 1], FP32, scratch)
        scratch.close()

        w0_stage = sb("w0_stage", [P, SPG, PARTS, HALVES * D], BF16)
        ib_stage = sb("ib_stage", [P, SPG, F], BF16)
        ob_stage = sb("ob_stage", [P, SPG, D], BF16)
        pick_stage = sb("pick_stage", [P, SPG, PARTS * P], BF16)
        w2_parts = sb("w2_parts", [P, SPG, PARTS, HALVES * D], BF16)
        x_parts = sb("x_parts", [P, PARTS, HALVES, GT], BF16)
        x_rest = sb("x_rest", [P, HALVES, GT])
        x_bias = sb("x_bias", [P, HALVES, GT])
        y0 = sb("y0", [P, HALVES, GT])
        y0_cos = sb("y0_cos", [P, HALVES, GT])
        y0_sin = sb("y0_sin", [P, HALVES, GT])
        y1 = sb("y1", [P, HALVES, GT])
        y1_rest = sb("y1_rest", [P, HALVES, GT])
        y1_parts = sb("y1_parts", [P, PARTS, HALVES, GT], BF16)
        y1_bias = sb("y1_bias", [P, HALVES, GT])
        y2 = sb("y2", [P, 2, HALVES, GT])
        low_parts = sb("low_parts", [P, PARTS, GT], BF16)
        low_rest = sb("low_rest", [P, GT])
        stack = sb("stack", [P, GT], BF16)
        y3 = sb("y3", [P, HALVES, GT])

        banks = [ctx.enter_context(nc.psum_tensor(f"bank{n}", [P, 512], FP32)) for n in range(8)]

        def halves(bank):
            return bank[:, :].rearrange("p (h t) -> p h t", h=HALVES)

        turn_bank = banks[0]
        front_bank = banks[1]
        hidden_banks = banks[2:5]
        out_bank = banks[5]
        low_bank = banks[6]
        stack_bank = banks[7]
        HIDDEN_BANK = [hidden_banks[k % 3] for k in range(PAIRS)]

        in_ident = sem("in_ident")
        in_index = sem("in_index")
        in_rot = sem("in_rot")
        in_lora_a = sem("in_lora_a")
        in_lora_b = sem("in_lora_b")
        in_common = sem("in_common")
        in_wi = sem("in_wi")
        in_wo = sem("in_wo")
        in_bias = sem("in_bias")
        in_w0 = [sem("in_w0_0"), sem("in_w0_1")]
        rot_step = sem("rot_step")
        rot_angles = sem("rot_angles")
        rot_power = sem("rot_power")
        rot_trig = sem("rot_trig")
        rot_saved = sem("rot_saved")
        pick_done = sem("pick_done")
        hot_step = sem("hot_step")
        hot_done = sem("hot_done")
        common_scaled = sem("common_scaled")
        pre_full = sem("pre_full")
        pre_high = sem("pre_high")
        pre_rest = sem("pre_rest")
        pre_low = sem("pre_low")
        pre_step = sem("pre_step")
        exp_full = sem("exp_full")
        exp_w0_full = sem("exp_w0_full")
        exp_w0_high = sem("exp_w0_high")
        exp_w0_rest = sem("exp_w0_rest")
        exp_w0_mid = sem("exp_w0_mid")
        exp_w0_low = sem("exp_w0_low")
        exp_act = sem("exp_act")
        exp_dve = sem("exp_dve")
        pre_pe_done = sem("pre_pe_done")

        x_in = sem("x_in")
        rotation_in = sem("rotation_in")
        w2_in = [sem(f"w2_in{s}") for s in range(SPG)]
        out_stored = sem("out_stored")
        x_turned = sem("x_turned")
        l0_full = sem("l0_full")
        l2_full = sem("l2_full")
        low1_full = sem("low1_full")
        low2_full = sem("low2_full")
        stack1_full = sem("stack1_full")
        stack2_full = sem("stack2_full")
        hidden_full = [sem(f"hidden_full{k}") for k in range(PAIRS)]
        out_full = sem("out_full")
        out_turned = sem("out_turned")
        x_high = sem("x_high")
        x_rested = sem("x_rested")
        x_biased = sem("x_biased")
        x_mid = sem("x_mid")
        x_split = sem("x_split")
        y0_done = sem("y0_done")
        y0_cos_done = sem("y0_cos_done")
        y0_sin_done = sem("y0_sin_done")
        y1_done = sem("y1_done")
        y1_high = sem("y1_high")
        y1_rested = sem("y1_rested")
        y1_mid = sem("y1_mid")
        y1_split = sem("y1_split")
        y1_biased = sem("y1_biased")
        y2_done = sem("y2_done")
        y2_high = sem("y2_high")
        y2_split = sem("y2_split")
        low1_high, low1_rested, low1_mid, low1_split = (sem(f"low1_{n}") for n in ("high", "rested", "mid", "split"))
        low2_high, low2_rested, low2_mid, low2_split = (sem(f"low2_{n}") for n in ("high", "rested", "mid", "split"))
        stack1_done = sem("stack1_done")
        stack2_done = sem("stack2_done")
        hid_high = [sem(f"hid_high{k}") for k in range(PAIRS)]
        hid_split = [sem(f"hid_split{k}") for k in range(PAIRS)]
        y3_done = sem("y3_done")
        out_taken = sem("out_taken")
        w2_high = [sem(f"w2_high{s}") for s in range(SPG)]
        w2_rested = [sem(f"w2_rested{s}") for s in range(SPG)]
        w2_mid = [sem(f"w2_mid{s}") for s in range(SPG)]
        w2_split = [sem(f"w2_split{s}") for s in range(SPG)]
        w0_staged = sem("w0_staged")
        ib_staged = sem("ib_staged")
        ob_staged = sem("ob_staged")
        pick_staged = sem("pick_staged")

        SPLIT2, SPLIT3, COPY = "two float32r parts", "three bfloat16 parts", "a copy"
        JOBS = []
        JOBS.append((SPLIT2, "ia", 0))
        JOBS += [(SPLIT2, "oa", n) for n in range(2)]
        JOBS += [(SPLIT3, "ib", n) for n in range(2)]
        JOBS.append((SPLIT3, "ob", 0))
        JOBS += [(COPY, "cib", n) for n in range(2)]
        JOBS.append((COPY, "cob", 0))
        JOBS.append((COPY, "bias", 0))
        JOBS += [(SPLIT2, "wi", n) for n in range(4)]
        JOBS += [(SPLIT2, "wo", n) for n in range(FT // 2)]
        HIGHS = [j + 1 for j in range(len(JOBS))]
        RESTS = [sum(JOBS[i][0] != COPY for i in range(j + 1)) for j in range(len(JOBS))]

        def job_views(j):
            how, name, n = JOBS[j]
            bank = banks[j % 8]
            if name == "ia":
                return bank[:, 0:256].rearrange("p (h e) -> p h e", h=HALVES), (ia_hi[:], ia_lo[:])
            if name == "oa":
                t = slice(4 * n, 4 * n + 4)
                return bank[:, :].rearrange("p (k e) -> p k e", k=4), (oa_hi[:, t, :], oa_lo[:, t, :])
            if name == "ib":
                return bank[:, :], [ib_parts[:, q, 512 * n:512 * (n + 1)] for q in range(PARTS)]
            if name == "ob":
                return bank[:, 0:D], [ob_parts[:, q, :] for q in range(PARTS)]
            if name == "cib":
                return bank[0:RANK, :], (cib_t[:, 512 * n:512 * (n + 1)],)
            if name == "cob":
                return bank[0:RANK, 0:D], (cob_t[:, :],)
            if name == "bias":
                return bank[:, :].rearrange("p (h b) -> p h b", h=2 * HALVES), (bias[:],)
            if name == "wi":
                k, c = n // 2, slice(512 * (n % 2), 512 * (n % 2) + 512)
                return bank[:, :], (wi_hi[:, k, c], wi_lo[:, k, c])
            if name == "wo":
                t = slice(2 * n, 2 * n + 2)
                return bank[:, :].rearrange("p (k d) -> p k d", k=2), (wo_hi[:, t, :], wo_lo[:, t, :])

        block = ctx.enter_context(nc.Block())

        @block.sync
        def _(sp):
            sp.dma_start(index[:, 0, :], experts.rearrange("(o b) -> o b", o=1)).then_inc(in_index, 16)
            sp.dma_start(index[:, 1, :], cats.rearrange("(o b) -> o b", o=1)).then_inc(in_index, 16)
            sp.dma_start(dt_sb[:], delta_t.rearrange("(b o) -> b o", o=1)).then_inc(in_rot, 16)
            sp.dma_start(rot[:, 0, :], amplitudes.partition_broadcast(P)).then_inc(in_rot, 16)
            sp.dma_start(rot[:, 1, :], frequencies.partition_broadcast(P)).then_inc(in_rot, 16)
            sp.dma_start(ident[:], identity).then_inc(in_ident, 16)
            sp.dma_start(ia_nat[:], experts_wi_a.rearrange("e r d -> (e r) d")).then_inc(in_lora_a, 16)
            sp.dma_start(oa_nat[:], experts_wo_a.rearrange("e r f -> (e r) f")).then_inc(in_lora_a, 16)
            for e in range(EXPERTS):
                columns = slice(RANK * e, RANK * (e + 1))
                sp.dma_start(ib_nat[:, :, columns],
                             experts_wi_b[e].rearrange("(t p) r -> p t r", p=P)).then_inc(in_lora_b, 16)
                sp.dma_start(ob_nat[:, :, columns],
                             experts_wo_b[e].rearrange("(t p) r -> p t r", p=P)).then_inc(in_lora_b, 16)
            sp.dma_start(x_sb[:], x_rows[0]).then_inc(x_in, 16)

            def load_w2(q, s):
                category = sp.value_load(index[0:1, 1, bass.ds(SPG * q + s, 1)], min_val=0, max_val=CATEGORIES - 1)
                sp.dma_start(w2_raw[:, s, :].rearrange("p (h d) -> p h d", h=HALVES),
                             w2[bass.ds(category, 1)].rearrange("o (h p) d -> p (o h) d", p=P)
                             ).then_inc(w2_in[s], 16)

            def load_rotation(q):
                sp.dma_start(rotation[:], rotation_dram[:, bass.ds(GT * q, GT)].partition_broadcast(P)
                             ).then_inc(rotation_in, 16)

            sp.wait_ge(in_index, 32)
            for s in range(SPG):
                load_w2(0, s)
            sp.wait_ge(rot_trig, 1)
            sp.dma_start(rotation_dram[0].rearrange("(b s) -> b s", s=SEQ), rot[:, 12, :]).then_inc(rot_saved, 16)
            sp.dma_start(rotation_dram[1].rearrange("(b s) -> b s", s=SEQ), rot[:, 13, :]).then_inc(rot_saved, 16)
            sp.wait_ge(rot_saved, 32)
            load_rotation(0)

            def ahead(g, q):
                sp.wait_ge(x_turned, q)
                sp.dma_start(x_sb[:], x_rows[bass.ds(q, 1)].rearrange("o p t d -> p (o t) d")).then_inc(x_in, 16)
                for s in range(SPG):
                    sp.wait_ge(w2_split[s], q)
                    load_w2(q, s)
                sp.wait_ge(y0_sin_done, q)
                load_rotation(q)

            def store(g):
                sp.wait_ge(out_taken, g + 2)
                sp.dma_start(out_rows[bass.ds(g, 1)].rearrange("o p t d -> p (o t) d"), out_sb[:]
                             ).then_inc(out_stored, 16)

            ahead(-1, 1)
            with sp.Fori(0, GROUPS - 2) as g:
                ahead(g, g + 2)
                store(g)
            store(GROUPS - 2)
            store(GROUPS - 1)
            sp.wait_ge(out_stored, 16 * (GROUPS + 1))

        @block.gpsimd
        def _(pool):
            pool.wait_ge(in_rot, 48)
            nc.gpsimd.tensor_tensor(rot[:, 2, :], rot[:, 0, :], dt_sb[:, 0:1].to_broadcast([P, SEQ]),
                                    ALU.pow).then_inc(rot_power, 1)

            def w2_take_high(q):
                for s in range(SPG):
                    pool.wait_ge(w2_high[s], q + 1)
                    nc.gpsimd.tensor_tensor(w2_raw[:, s, :], w2_raw[:, s, :], w2_parts[:, s, 0, :],
                                            ALU.subtract).then_inc(w2_rested[s], 1)

            def w2_take_mid(q):
                for s in range(SPG):
                    pool.wait_ge(w2_mid[s], q + 1)
                    nc.gpsimd.tensor_tensor(w2_parts[:, s, 2, :], w2_raw[:, s, :], w2_parts[:, s, 1, :],
                                            ALU.subtract).then_inc(w2_split[s], 1)

            def add_bias2(q):
                pool.wait_ge(y1_done, q + 1)
                b = bias[:, HALVES:2 * HALVES, bass.ds(SPG * q, SPG)].unsqueeze(3)
                nc.gpsimd.tensor_tensor(y1_bias[:].rearrange("p h (s t) -> p h s t", s=SPG),
                                        y1[:].rearrange("p h (s t) -> p h s t", s=SPG),
                                        b.to_broadcast([P, HALVES, SPG, SEQ]), ALU.add).then_inc(y1_biased, 1)

            w2_take_high(0)
            w2_take_mid(0)
            add_bias2(0)
            w2_take_high(1)
            with pool.Fori(0, GROUPS - 2) as g:
                w2_take_mid(g + 1)
                add_bias2(g + 1)
                w2_take_high(g + 2)
            w2_take_mid(GROUPS - 1)
            add_bias2(GROUPS - 1)

        @block.scalar
        def _(act):
            act.dma_start(small_sb[:], small).then_inc(in_bias, 16)
            act.dma_start(index_all[:, 0, :], experts.partition_broadcast(CATEGORIES)).then_inc(in_bias, 16)
            act.dma_start(index_all[:, 1, :], cats.partition_broadcast(CATEGORIES)).then_inc(in_bias, 16)
            act.dma_start(b0_nat[:], b0).then_inc(in_bias, 16)
            act.dma_start(b2_nat[:], b2).then_inc(in_bias, 16)
            act.dma_start(place_sb[:], place).then_inc(in_bias, 16)
            act.dma_start(cia[:], common_wi_a).then_inc(in_common, 16)
            act.dma_start(coa[:], common_wo_a).then_inc(in_common, 16)
            act.dma_start(cib_nat[:], common_wi_b.rearrange("(t p) r -> p t r", p=P)).then_inc(in_common, 16)
            act.dma_start(cob_nat[:], common_wo_b.rearrange("(t p) r -> p t r", p=P)).then_inc(in_common, 16)
            act.dma_start(wi_nat[:], wi.rearrange("(t p) d -> p t d", p=P)).then_inc(in_wi, 16)
            act.dma_start(wo_nat[:], wo.rearrange("(t p) f -> p t f", p=P)).then_inc(in_wo, 16)

            def load_w0(e, slot):
                act.dma_start(w0_nat[:, slot], w0[bass.ds(e, 1)].rearrange("o (h p) d -> p (o h) d", p=P)
                              ).then_inc(in_w0[slot], 16)

            load_w0(0, 0)
            load_w0(1, 1)
            act.wait_ge(rot_angles, 1)
            nc.scalar.activation(rot[:, 10, :], rot[:, 8, :], ACT.Sin)
            nc.scalar.activation(rot[:, 11, :], rot[:, 9, :], ACT.Sin).then_inc(rot_step, 100)
            act.wait_ge(in_common, 64)
            nc.scalar.mul(cia2[:], cia[:], ALPHA)
            nc.scalar.mul(coa2[:], coa[:], ALPHA).then_inc(common_scaled, 1)

            for j, (how, name, n) in enumerate(JOBS):
                bank, parts = job_views(j)
                act.wait_ge(pre_full, j + 1)
                nc.scalar.copy(parts[0], bank).then_inc(pre_high, 1)

            def two_experts(t, more):
                act.wait_ge(exp_w0_full, t + 1)
                if more:
                    for i in range(2):
                        load_w0(2 * t + 2 + i, i)
                for i in range(2):
                    nc.scalar.copy(w0_parts[:, bass.ds(2 * t + i, 1), 0, :].rearrange("p o c -> p (o c)"),
                                   banks[i][:, :]).then_inc(exp_w0_high, 1)
                for i in range(2):
                    act.wait_ge(exp_w0_rest, 2 * t + i + 1)
                    nc.scalar.copy(w0_parts[:, bass.ds(2 * t + i, 1), 1, :].rearrange("p o c -> p (o c)"),
                                   rest[:, i, :]).then_inc(exp_w0_mid, 1)
                act.wait_ge(exp_full, t + 1)
                for i in range(2):
                    nc.scalar.copy(ib_stack[:, bass.ds(2 * t + i, 1), 0:512].rearrange("p o c -> p (o c)"),
                                   banks[2 + 2 * i][:, :])
                nc.scalar.copy(ob_stack[:, bass.ds(2 * t, 2), :].rearrange("p o c -> p (o c)"),
                               banks[6][:, :]).then_inc(exp_act, 1)

            with act.Fori(0, EXPERTS // 2 - 1) as t:
                two_experts(t, True)
            two_experts(EXPERTS // 2 - 1, False)

            def x_take_high(q):
                act.wait_ge(x_turned, q + 1)
                nc.scalar.copy(x_parts[:, 0], halves(turn_bank)).then_inc(x_high, 1)

            def x_take_mid(q):
                act.wait_ge(x_rested, q + 1)
                nc.scalar.copy(x_parts[:, 1], x_rest[:]).then_inc(x_mid, 1)

            def y1_take_high(q):
                act.wait_ge(y1_done, q + 1)
                nc.scalar.copy(y1_parts[:, 0], y1[:]).then_inc(y1_high, 1)

            def y1_take_mid(q):
                act.wait_ge(y1_rested, q + 1)
                nc.scalar.copy(y1_parts[:, 1], y1_rest[:]).then_inc(y1_mid, 1)

            def y2_take_high(q):
                act.wait_ge(y2_done, q + 1)
                nc.scalar.copy(y2_hi[:], y2[:, bass.ds(q % 2, 1)].rearrange("p o h t -> p (o h) t")
                               ).then_inc(y2_high, 1)

            def low_take_high(q, full, high):
                act.wait_ge(full, q + 1)
                nc.scalar.copy(low_parts[:, 0], low_bank[:, 0:GT]).then_inc(high, 1)

            def low_take_mid(q, rested, mid):
                act.wait_ge(rested, q + 1)
                nc.scalar.copy(low_parts[:, 1], low_rest[:]).then_inc(mid, 1)

            def take_stack(q, full, done):
                act.wait_ge(full, q + 1)
                nc.scalar.copy(stack[:], stack_bank[:, 0:GT]).then_inc(done, 1)

            def hidden_take_high(g, k):
                act.wait_ge(hidden_full[k], g + 1)
                nc.scalar.activation(hid_hi[:, 2 * k:2 * k + 2, :], halves(HIDDEN_BANK[k]), ACT.Relu
                                     ).then_inc(hid_high[k], 1)

            def w2_take_high(q):
                for s in range(SPG):
                    act.wait_ge(w2_in[s], 16 * q + 16)
                    nc.scalar.copy(w2_parts[:, s, 0, :], w2_raw[:, s, :]).then_inc(w2_high[s], 1)

            def w2_take_mid(q):
                for s in range(SPG):
                    act.wait_ge(w2_rested[s], q + 1)
                    nc.scalar.copy(w2_parts[:, s, 1, :], w2_raw[:, s, :]).then_inc(w2_mid[s], 1)

            def take_out(g):
                act.wait_ge(out_turned, g + 1)
                act.wait_ge(out_stored, 16 * g + 16)
                nc.scalar.copy(out_sb[:], turn_bank[:, :].rearrange("p (t d) -> p t d", t=TILES)
                               ).then_inc(out_taken, 1)

            def body(g, front, further):
                n = g + 1
                if front:
                    x_take_high(n)
                    x_take_mid(n)
                hidden_take_high(g, 0)
                hidden_take_high(g, 1)
                hidden_take_high(g, 2)
                if front:
                    w2_take_mid(n)
                hidden_take_high(g, 3)
                if front:
                    y1_take_high(n)
                    y1_take_mid(n)
                low_take_high(g, low2_full, low2_high)
                low_take_mid(g, low2_rested, low2_mid)
                if front:
                    y2_take_high(n)
                take_stack(g, stack2_full, stack2_done)
                if further:
                    act.wait_ge(l2_full, n + 1)
                    w2_take_high(n + 1)
                if front:
                    low_take_high(n, low1_full, low1_high)
                    low_take_mid(n, low1_rested, low1_mid)
                take_out(g)
                if front:
                    take_stack(n, stack1_full, stack1_done)

            act.wait_ge(pre_pe_done, 1)
            act.wait_ge(exp_dve, EXPERTS // 2)
            act.sem_inc(out_taken, 1)
            act.sem_inc(out_stored, 16)
            w2_take_high(0)
            x_take_high(0)
            x_take_mid(0)
            w2_take_mid(0)
            y1_take_high(0)
            y1_take_mid(0)
            y2_take_high(0)
            act.wait_ge(l2_full, 1)
            w2_take_high(1)
            low_take_high(0, low1_full, low1_high)
            low_take_mid(0, low1_rested, low1_mid)
            take_stack(0, stack1_full, stack1_done)
            with act.Fori(0, GROUPS - 2) as g:
                body(g, True, True)
            body(GROUPS - 2, True, False)
            body(GROUPS - 1, False, False)

        @block.vector
        def _(dve):
            steps = [0]

            def then(instruction):
                steps[0] += 1
                instruction.then_inc(pre_step, 1)
                dve.wait_ge(pre_step, steps[0])

            TWO_PI = 2.0 * np.pi
            ROUND = 1.5 * 2.0 ** 23
            C1 = 6.28125
            C2 = float(np.float32(np.round((TWO_PI - C1) * 2.0 ** 21) / 2.0 ** 21))
            C3 = float(np.float32(TWO_PI - C1 - C2))
            LIMIT = 3.1415925
            dve.wait_ge(in_rot, 48)
            then(nc.vector.tensor_scalar(rot[:, 3, :], rot[:, 1, :], dt_sb[:, 0:1], None, ALU.mult))
            for at, offset, shift in ((4, 0.0, 0.0), (5, 0.25, 0.5 * np.pi)):
                angle = 8 if at == 4 else 9
                then(nc.vector.tensor_scalar(rot[:, at, :], rot[:, 3, :], float(1.0 / TWO_PI), offset, ALU.mult, ALU.add))
                then(nc.vector.tensor_scalar(rot[:, 6, :], rot[:, at, :], ROUND, None, ALU.add))
                then(nc.vector.tensor_scalar(rot[:, 7, :], rot[:, 6, :], -ROUND, None, ALU.add))
                then(nc.vector.scalar_tensor_tensor(rot[:, at, :], rot[:, 7, :], -C1, rot[:, 3, :], ALU.mult, ALU.add))
                then(nc.vector.scalar_tensor_tensor(rot[:, 6, :], rot[:, 7, :], -C2, rot[:, at, :], ALU.mult, ALU.add))
                then(nc.vector.scalar_tensor_tensor(rot[:, at, :], rot[:, 7, :], -C3, rot[:, 6, :], ALU.mult, ALU.add))
                then(nc.vector.tensor_scalar(rot[:, 6, :], rot[:, at, :], shift, LIMIT, ALU.add, ALU.min))
                then(nc.vector.tensor_scalar(rot[:, angle, :], rot[:, 6, :], -LIMIT, None, ALU.max))
            nc.vector.memset(rot[0:1, 7, 0:1], 0.0).then_inc(rot_angles, 1)
            dve.wait_ge(in_bias, 96)
            then(nc.vector.tensor_copy(index_f[:], index_all[:]))
            nc.vector.tensor_scalar(one_hot[:], index_f[:], small_sb[0:CATEGORIES, 0:1], None, ALU.is_equal).then_inc(hot_done, 1)
            for e in range(EXPERTS):
                nc.vector.tensor_scalar(pick[:, e, :], place_sb[:, 0, :], small_sb[:, 1 + e:2 + e], ALPHA, ALU.mult, ALU.mult)
                last = nc.vector.tensor_scalar(put[:, e, :], place_sb[:, 1, :], small_sb[:, 1 + e:2 + e], None, ALU.mult)
            last.then_inc(pick_done, 1)
            dve.wait_ge(rot_power, 1)
            dve.wait_ge(rot_step, 100)
            then(nc.vector.tensor_tensor(rot[:, 4, :], rot[:, 2, :], rot[:, 11, :], ALU.mult))
            nc.vector.tensor_scalar(rot[:, 12, :], rot[:, 4, :], 1.0, None, ALU.add)
            nc.vector.tensor_tensor(rot[:, 13, :], rot[:, 2, :], rot[:, 10, :], ALU.mult).then_inc(rot_trig, 1)

            rests = 0
            for j, (how, name, n) in enumerate(JOBS):
                if how == COPY:
                    continue
                bank, parts = job_views(j)
                dve.wait_ge(pre_high, HIGHS[j])
                if how == SPLIT2:
                    nc.vector.tensor_tensor(parts[1], bank, parts[0], ALU.subtract).then_inc(pre_rest, 1)
                    rests += 1
                else:
                    width = 512 if name == "ib" else D
                    room = rest[:, 0, 0:width]
                    nc.vector.tensor_tensor(room, bank, parts[0], ALU.subtract).then_inc(pre_rest, 1)
                    rests += 1
                    dve.wait_ge(pre_rest, rests)
                    then(nc.vector.tensor_copy(parts[1], room))
                    then(nc.vector.tensor_tensor(parts[2], room, parts[1], ALU.subtract))
            nc.vector.memset(rest[0:1, 1, 0:1], 0.0).then_inc(pre_low, 1)

            with dve.Fori(0, EXPERTS // 2) as t:
                for i in range(2):
                    dve.wait_ge(exp_w0_high, 2 * t + i + 1)
                    nc.vector.tensor_tensor(rest[:, i, :], banks[i][:, :],
                                            w0_parts[:, bass.ds(2 * t + i, 1), 0, :].rearrange("p o c -> p (o c)"),
                                            ALU.subtract).then_inc(exp_w0_rest, 1)
                for i in range(2):
                    dve.wait_ge(exp_w0_mid, 2 * t + i + 1)
                    nc.vector.tensor_tensor(w0_parts[:, bass.ds(2 * t + i, 1), 2, :].rearrange("p o c -> p (o c)"),
                                            rest[:, i, :],
                                            w0_parts[:, bass.ds(2 * t + i, 1), 1, :].rearrange("p o c -> p (o c)"),
                                            ALU.subtract).then_inc(exp_w0_low, 1)
                dve.wait_ge(exp_full, t + 1)
                dve.wait_ge(exp_w0_low, 2 * t + 2)
                for i in range(2):
                    last = nc.vector.tensor_copy(ib_stack[:, bass.ds(2 * t + i, 1), 512:1024].rearrange("p o c -> p (o c)"),
                                                 banks[3 + 2 * i][:, :])
                last.then_inc(exp_dve, 1)

            def expert(q, s):
                return dve.value_load(index[0:1, 0, bass.ds(SPG * q + s, 1)], min_val=0, max_val=EXPERTS - 1)

            def stage(q, table, room, staged):
                for s in range(SPG):
                    e = expert(q, s)
                    last = nc.vector.tensor_copy(room(s), table(e))
                last.then_inc(staged, 1)

            def stage_w0(q):
                stage(q, lambda e: w0_parts[:, bass.ds(e, 1)].rearrange("p o k c -> p (o k c)"),
                      lambda s: w0_stage[:, s].rearrange("p k c -> p (k c)"), w0_staged)

            def stage_ib(q):
                stage(q, lambda e: ib_stack[:, bass.ds(e, 1), :].rearrange("p o c -> p (o c)"),
                      lambda s: ib_stage[:, s, :], ib_staged)

            def stage_ob(q):
                stage(q, lambda e: ob_stack[:, bass.ds(e, 1), :].rearrange("p o c -> p (o c)"),
                      lambda s: ob_stage[:, s, :], ob_staged)

            def stage_pick(q):
                stage(q, lambda e: pick[:, bass.ds(e, 1), :].rearrange("p o c -> p (o c)"),
                      lambda s: pick_stage[:, s, :], pick_staged)

            def x_take_rest(q):
                dve.wait_ge(x_high, q + 1)
                nc.vector.tensor_tensor(x_rest[:], halves(turn_bank), x_parts[:, 0], ALU.subtract).then_inc(x_rested, 1)
                b = bias[:, 0:HALVES, bass.ds(SPG * q, SPG)].unsqueeze(3)
                nc.vector.tensor_tensor(x_bias[:].rearrange("p h (s t) -> p h s t", s=SPG),
                                        turn_bank[:, :].rearrange("p (h s t) -> p h s t", h=HALVES, s=SPG),
                                        b.to_broadcast([P, HALVES, SPG, SEQ]), ALU.add).then_inc(x_biased, 1)

            def x_take_low(q):
                dve.wait_ge(x_mid, q + 1)
                nc.vector.tensor_tensor(x_parts[:, 2], x_rest[:], x_parts[:, 1], ALU.subtract).then_inc(x_split, 1)

            def hidden_take_low(g, k):
                dve.wait_ge(hid_high[k], g + 1)
                nc.vector.scalar_tensor_tensor(hid_lo[:, 2 * k:2 * k + 2, :], halves(HIDDEN_BANK[k]), 0.0,
                                               hid_hi[:, 2 * k:2 * k + 2, :], ALU.max, ALU.subtract
                                               ).then_inc(hid_split[k], 1)

            def l0_sum(q):
                dve.wait_ge(l0_full, q + 1)
                dve.wait_ge(x_biased, q + 1)
                nc.vector.tensor_tensor(y0[:], halves(front_bank), x_bias[:], ALU.add).then_inc(y0_done, 1)

            def rotate(q):
                dve.wait_ge(rotation_in, 16 * q + 16)
                dve.wait_ge(y0_done, q + 1)
                nc.vector.tensor_tensor(y0_cos[:], y0[:], rotation[:, 0, :].unsqueeze(1).to_broadcast([P, HALVES, GT]),
                                        ALU.mult).then_inc(y0_cos_done, 1)
                nc.vector.tensor_tensor(y0_sin[:], y0[:], rotation[:, 1, :].unsqueeze(1).to_broadcast([P, HALVES, GT]),
                                        ALU.mult).then_inc(y0_sin_done, 1)

            def rotate_sum(q):
                dve.wait_ge(y0_cos_done, q + 1)
                dve.wait_ge(y0_sin_done, q + 1)
                nc.vector.tensor_tensor(y1[:, 0], y0_cos[:, 0], y0_sin[:, 1], ALU.subtract)
                nc.vector.tensor_tensor(y1[:, 1], y0_sin[:, 0], y0_cos[:, 1], ALU.add).then_inc(y1_done, 1)

            def y1_take_rest(q):
                dve.wait_ge(y1_high, q + 1)
                nc.vector.tensor_tensor(y1_rest[:], y1[:], y1_parts[:, 0], ALU.subtract).then_inc(y1_rested, 1)

            def y1_take_low(q):
                dve.wait_ge(y1_mid, q + 1)
                nc.vector.tensor_tensor(y1_parts[:, 2], y1_rest[:], y1_parts[:, 1], ALU.subtract).then_inc(y1_split, 1)

            def low_take_rest(q, high, rested):
                dve.wait_ge(high, q + 1)
                nc.vector.tensor_tensor(low_rest[:], low_bank[:, 0:GT], low_parts[:, 0], ALU.subtract).then_inc(rested, 1)

            def low_take_low(q, mid, split):
                dve.wait_ge(mid, q + 1)
                nc.vector.tensor_tensor(low_parts[:, 2], low_rest[:], low_parts[:, 1], ALU.subtract).then_inc(split, 1)

            def l2_sum(q):
                dve.wait_ge(l2_full, q + 1)
                dve.wait_ge(y1_biased, q + 1)
                nc.vector.tensor_tensor(y2[:, bass.ds(q % 2, 1)].rearrange("p o h t -> p (o h) t"),
                                        halves(front_bank), y1_bias[:], ALU.add).then_inc(y2_done, 1)

            def y2_take_low(q):
                dve.wait_ge(y2_high, q + 1)
                nc.vector.tensor_tensor(y2_lo[:], y2[:, bass.ds(q % 2, 1)].rearrange("p o h t -> p (o h) t"),
                                        y2_hi[:], ALU.subtract).then_inc(y2_split, 1)

            def l3_sum(g):
                dve.wait_ge(out_full, g + 1)
                nc.vector.tensor_tensor(y3[:], halves(out_bank),
                                        y2[:, bass.ds(g % 2, 1)].rearrange("p o h t -> p (o h) t"),
                                        ALU.add).then_inc(y3_done, 1)

            def body(g, front, further):
                n = g + 1
                if front:
                    x_take_rest(n)
                    x_take_low(n)
                hidden_take_low(g, 0)
                hidden_take_low(g, 1)
                hidden_take_low(g, 2)
                if front:
                    l0_sum(n)
                    rotate(n)
                hidden_take_low(g, 3)
                if front:
                    rotate_sum(n)
                    y1_take_rest(n)
                low_take_rest(g, low2_high, low2_rested)
                if front:
                    y1_take_low(n)
                low_take_low(g, low2_mid, low2_split)
                if further:
                    stage_w0(n + 1)
                if front:
                    stage_ib(n)
                    l2_sum(n)
                    dve.wait_ge(stack2_full, g + 1)
                    y2_take_low(n)
                    stage_pick(n)
                    low_take_rest(n, low1_high, low1_rested)
                    low_take_low(n, low1_mid, low1_split)
                l3_sum(g)
                if front:
                    stage_ob(n)

            dve.wait_ge(in_index, 32)
            dve.wait_ge(pre_pe_done, 1)
            dve.wait_ge(exp_act, EXPERTS // 2)
            dve.wait_ge(exp_dve, EXPERTS // 2)
            stage_w0(0)
            x_take_rest(0)
            x_take_low(0)
            stage_pick(0)
            stage_ib(0)
            stage_ob(0)
            l0_sum(0)
            rotate(0)
            rotate_sum(0)
            y1_take_rest(0)
            y1_take_low(0)
            stage_w0(1)
            l2_sum(0)
            y2_take_low(0)
            low_take_rest(0, low1_high, low1_rested)
            low_take_low(0, low1_mid, low1_split)
            with dve.Fori(0, GROUPS - 2) as g:
                body(g, True, True)
            body(GROUPS - 2, True, False)
            body(GROUPS - 1, False, False)

        @block.tensor
        def _(pe):
            pe.wait_ge(in_ident, 16)

            def free(j):
                if j >= 8:
                    pe.wait_ge(pre_high, HIGHS[j - 8])
                    pe.wait_ge(pre_rest, RESTS[j - 8])

            arrived = {
                "ia": (in_lora_a, 32), "ib": (in_lora_b, 16 * 2 * EXPERTS), "cib": (in_common, 64),
                "wi": (in_wi, 16), "wo": (in_wo, 16), "bias": (in_bias, 96),
            }
            for j, (how, name, n) in enumerate(JOBS):
                bank = banks[j % 8]
                free(j)
                if name in arrived and n == 0:
                    pe.wait_ge(*arrived[name])
                if name == "ia":
                    for h in range(HALVES):
                        last = nc.tensor.transpose(bank[:, P * h:P * (h + 1)], ia_nat[:, P * h:P * (h + 1)], ident[:])
                if name == "oa":
                    for i in range(4):
                        t = 4 * n + i
                        last = nc.tensor.transpose(bank[:, P * i:P * (i + 1)], oa_nat[:, P * t:P * (t + 1)], ident[:])
                if name == "ib":
                    for i in range(4):
                        last = nc.tensor.transpose(bank[:, P * i:P * (i + 1)], ib_nat[:, 4 * n + i, :], ident[:])
                if name == "ob":
                    for h in range(HALVES):
                        last = nc.tensor.transpose(bank[:, P * h:P * (h + 1)], ob_nat[:, h, :], ident[:])
                if name == "cib":
                    for i in range(4):
                        last = nc.tensor.transpose(bank[0:RANK, P * i:P * (i + 1)], cib_nat[:, 4 * n + i, :], ident[:])
                if name == "cob":
                    for h in range(HALVES):
                        last = nc.tensor.transpose(bank[0:RANK, P * h:P * (h + 1)], cob_nat[:, h, :], ident[:])
                if name == "bias":
                    pe.wait_ge(hot_done, 1)
                    for layer, (table, rows) in enumerate(((b0_nat, EXPERTS), (b2_nat, CATEGORIES))):
                        for h in range(HALVES):
                            c = BATCH * (HALVES * layer + h)
                            last = nc.tensor.matmul(bank[:, c:c + BATCH], table[0:rows, P * h:P * (h + 1)],
                                                    one_hot[0:rows, layer, :], start=True, stop=True)
                if name == "wi":
                    k, half = n // 2, n % 2
                    if n == 0:
                        pe.wait_ge(common_scaled, 1)
                        pe.wait_ge(pre_high, HIGHS[[i for i, job in enumerate(JOBS) if job[1] == "cob"][0]])
                    nc.tensor.matmul(bank[:, :], cia2[:, P * k:P * (k + 1)], cib_t[:, 512 * half:512 * half + 512],
                                     start=True, stop=True, skip_group_check=True)
                    for i in range(4):
                        last = nc.tensor.matmul(bank[:, P * i:P * (i + 1)], wi_nat[:, 4 * half + i, P * k:P * (k + 1)],
                                                ident[:], start=False, stop=True, skip_group_check=True)
                if name == "wo":
                    for i in range(2):
                        t = 2 * n + i
                        nc.tensor.matmul(bank[:, D * i:D * (i + 1)], coa2[:, P * t:P * (t + 1)], cob_t[:],
                                         start=True, stop=True, skip_group_check=True)
                        for h in range(HALVES):
                            last = nc.tensor.matmul(bank[:, D * i + P * h:D * i + P * (h + 1)],
                                                    wo_nat[:, h, P * t:P * (t + 1)], ident[:],
                                                    start=False, stop=True, skip_group_check=True)
                last.then_inc(pre_full, 1)

            pe.wait_ge(pre_high, len(JOBS))
            pe.wait_ge(pre_rest, RESTS[-1])
            pe.wait_ge(pre_low, 1)
            pe.wait_ge(pick_done, 1)
            with pe.Fori(0, EXPERTS // 2) as t:
                for i in range(2):
                    pe.wait_ge(in_w0[i], 16 * t + 16)
                for i in range(2):
                    for k in range(HALVES):
                        for h in range(HALVES):
                            last = nc.tensor.transpose(banks[i][:, D * k + P * h:D * k + P * (h + 1)],
                                                       w0_nat[:, i, h, P * k:P * (k + 1)], ident[:])
                last.then_inc(exp_w0_full, 1)
                for i in range(2):
                    select = put[:, bass.ds(2 * t + i, 1), :].rearrange("p o c -> p (o c)")
                    for half in range(2):
                        for part in range(PARTS):
                            nc.tensor.matmul(banks[2 + 2 * i + half][:, :], select[:, P * part:P * (part + 1)],
                                             ib_parts[:, part, 512 * half:512 * half + 512],
                                             start=(part == 0), stop=(part == PARTS - 1))
                for i in range(2):
                    select = put[:, bass.ds(2 * t + i, 1), :].rearrange("p o c -> p (o c)")
                    for part in range(PARTS):
                        last = nc.tensor.matmul(banks[6][:, D * i:D * (i + 1)], select[:, P * part:P * (part + 1)],
                                                ob_parts[:, part, :], start=(part == 0), stop=(part == PARTS - 1))
                last.then_inc(exp_full, 1)
                pe.wait_ge(exp_w0_rest, 2 * t + 2)
                pe.wait_ge(exp_act, t + 1)
                pe.wait_ge(exp_dve, t + 1)
                pe.nop()
            nc.tensor.transpose(banks[0][:, 0:P], ident[:], ident[:]).then_inc(pre_pe_done, 1)

            def turn_x(q):
                pe.wait_ge(x_in, 16 * q + 16)
                if not isinstance(q, int) or q > 0:
                    pe.wait_ge(out_taken, q)
                for t in range(TILES):
                    for h in range(HALVES):
                        last = nc.tensor.transpose(halves(turn_bank)[:, h, P * t:P * (t + 1)],
                                                   x_sb[:, t, P * h:P * (h + 1)], ident[:])
                last.then_inc(x_turned, 1)

            def per_sample(weights, parts, full):
                for h in range(HALVES):
                    for s in range(SPG):
                        count = 0
                        for w_part, a_part in PRODUCTS:
                            for k in range(HALVES):
                                c = D * k + P * h
                                last = nc.tensor.matmul(halves(front_bank)[:, h, SEQ * s:SEQ * (s + 1)],
                                                        weights[:, s, w_part, c:c + P],
                                                        parts[:, a_part, k, SEQ * s:SEQ * (s + 1)],
                                                        start=(count == 0), stop=(count == 2 * len(PRODUCTS) - 1))
                                count += 1
                last.then_inc(full, 1)

            def l0(q):
                pe.wait_ge(x_split, q + 1)
                pe.wait_ge(w0_staged, q + 1)
                per_sample(w0_stage, x_parts, l0_full)

            def l2(q):
                pe.wait_ge(y1_split, q + 1)
                for s in range(SPG):
                    pe.wait_ge(w2_split[s], q + 1)
                per_sample(w2_parts, y1_parts, l2_full)

            def three(bank, w_hi, w_lo, a_hi, a_lo, start=False, stop=False):
                nc.tensor.matmul(bank, w_lo, a_hi, start=start, stop=False, skip_group_check=True)
                nc.tensor.matmul(bank, w_hi, a_lo, start=False, stop=False, skip_group_check=True)
                return nc.tensor.matmul(bank, w_hi, a_hi, start=False, stop=stop, skip_group_check=True)

            def low1(q):
                pe.wait_ge(y2_split, q + 1)
                for k in range(HALVES):
                    last = three(low_bank[:, 0:GT], ia_hi[:, k, :], ia_lo[:, k, :], y2_hi[:, k, :], y2_lo[:, k, :],
                                 start=(k == 0), stop=(k == HALVES - 1))
                last.then_inc(low1_full, 1)

            def low2(g):
                for k in range(FT):
                    if k % 2 == 0:
                        pe.wait_ge(hid_split[k // 2], g + 1)
                    last = three(low_bank[:, 0:GT], oa_hi[:, k, :], oa_lo[:, k, :], hid_hi[:, k, :], hid_lo[:, k, :],
                                 start=(k == 0), stop=(k == FT - 1))
                last.then_inc(low2_full, 1)

            def pick_stack(q, split, full):
                pe.wait_ge(split, q + 1)
                for s in range(SPG):
                    for part in range(PARTS):
                        last = nc.tensor.matmul(stack_bank[:, SEQ * s:SEQ * (s + 1)],
                                                pick_stage[:, s, P * part:P * (part + 1)],
                                                low_parts[:, part, SEQ * s:SEQ * (s + 1)],
                                                start=(part == 0), stop=(part == PARTS - 1))
                last.then_inc(full, 1)

            def hidden_base(k):
                for i in range(2):
                    f = 2 * k + i
                    for h in range(HALVES):
                        three(halves(HIDDEN_BANK[k])[:, i, :], wi_hi[:, h, P * f:P * (f + 1)],
                              wi_lo[:, h, P * f:P * (f + 1)], y2_hi[:, h, :], y2_lo[:, h, :],
                              start=(i == 0 and h == 0), stop=(h == HALVES - 1))

            def hidden_lora(k):
                for i in range(2):
                    f = 2 * k + i
                    for s in range(SPG):
                        last = nc.tensor.matmul(halves(HIDDEN_BANK[k])[:, i, SEQ * s:SEQ * (s + 1)],
                                                ib_stage[:, s, P * f:P * (f + 1)], stack[:, SEQ * s:SEQ * (s + 1)],
                                                start=False, stop=True, skip_group_check=True)
                last.then_inc(hidden_full[k], 1)

            def out_half(h):
                for k in range(FT):
                    three(halves(out_bank)[:, h, :], wo_hi[:, k, P * h:P * (h + 1)], wo_lo[:, k, P * h:P * (h + 1)],
                          hid_hi[:, k, :], hid_lo[:, k, :], start=(h == 0 and k == 0), stop=(k == FT - 1))

            def out_lora(g):
                pe.wait_ge(stack2_done, g + 1)
                pe.wait_ge(ob_staged, g + 1)
                for h in range(HALVES):
                    for s in range(SPG):
                        last = nc.tensor.matmul(halves(out_bank)[:, h, SEQ * s:SEQ * (s + 1)],
                                                ob_stage[:, s, P * h:P * (h + 1)], stack[:, SEQ * s:SEQ * (s + 1)],
                                                start=False, stop=True, skip_group_check=True)
                last.then_inc(out_full, 1)

            def turn_out(g, q):
                pe.wait_ge(y3_done, g + 1)
                pe.wait_ge(x_biased, q + 1)
                for t in range(TILES):
                    for h in range(HALVES):
                        last = nc.tensor.transpose(turn_bank[:, D * t + P * h:D * t + P * (h + 1)],
                                                   y3[:, h, P * t:P * (t + 1)], ident[:])
                last.then_inc(out_turned, 1)

            def body(g, front):
                n = g + 1
                if front:
                    turn_x(n)
                pe.wait_ge(stack1_done, g + 1)
                pe.wait_ge(ib_staged, g + 1)
                hidden_lora(0)
                hidden_lora(1)
                hidden_base(2)
                hidden_lora(2)
                if front:
                    l0(n)
                pe.wait_ge(hid_split[0], g + 1)
                hidden_base(3)
                hidden_lora(3)
                low2(g)
                out_half(0)
                if front:
                    l2(n)
                pick_stack(g, low2_split, stack2_full)
                out_half(1)
                if front:
                    low1(n)
                out_lora(g)
                if front:
                    hidden_base(0)
                turn_out(g, n if front else g)
                if front:
                    hidden_base(1)
                    pe.wait_ge(pick_staged, n + 1)
                    pick_stack(n, low1_split, stack1_full)

            turn_x(0)
            l0(0)
            l2(0)
            low1(0)
            hidden_base(0)
            hidden_base(1)
            pe.wait_ge(pick_staged, 1)
            pick_stack(0, low1_split, stack1_full)
            with pe.Fori(0, GROUPS - 1) as g:
                body(g, True)
            body(GROUPS - 1, False)


_INS = ['x', 'itok_B_0_7', 'condB_deltat', 'itok_B_0_63', 'L0_cond_weight', 'L0_cond_bias',
        'L1_cond_amplitudes', 'L1_cond_frequencies', 'L2_cond_W', 'L2_cond_b', 'L3_cond_wi', 'L3_cond_wo',
        'L3_cond_common_wi_a', 'L3_cond_common_wi_b', 'L3_cond_common_wo_a', 'L3_cond_common_wo_b',
        'L3_cond_experts_wi_a', 'L3_cond_experts_wi_b', 'L3_cond_experts_wo_a', 'L3_cond_experts_wo_b']
_OUT = ((BATCH, SEQ, D), 'float32')


def kernel(**inputs):
    import concourse.bacc as _bacc
    from concourse.bass_utils import run_bass_kernel_spmd as _run

    nc = _bacc.Bacc("TRN2", target_bir_lowering=False, num_devices=1)
    arrays, args = {}, []
    given = {name: np.ascontiguousarray(inputs[name]) for name in _INS}
    given["identity"] = np.eye(P, dtype=np.float32)
    given["place"] = stack_constants()
    given["small"] = small_constants()
    for name, a in given.items():
        arrays[f"in_{name}_dram"] = a
        args.append(nc.dram_tensor(f"in_{name}_dram", a.shape, mybir.dt.from_np(a.dtype), kind="ExternalInput").ap())
    args.append(nc.dram_tensor("out_0_dram", _OUT[0], FP32, kind="ExternalOutput").ap())
    cond_resid_kernel(nc, *args)
    r = _run(nc, [arrays], core_ids=[0])
    return r.results[0]["out_0_dram"]
```

```python
from contextlib import ExitStack

import numpy as np

import concourse.bass as bass
from concourse import mybir

FP32 = mybir.dt.float32
F32R = mybir.dt.float32r
BF16 = mybir.dt.bfloat16
I32 = mybir.dt.int32
ALU = mybir.AluOpType
ACT = mybir.ActivationFunctionType

P = 128
BATCH, SEQ, D = 128, 64, 256
F = 1024
EXPERTS, RANK = 8, 16
CATEGORIES = 64
SPG = 4
GT = SPG * SEQ
GROUPS = BATCH // SPG
TILES = GT // P
HALVES = D // P
FT = F // P
PAIRS = FT // 2
PARTS = 3
PRODUCTS = [(2, 0), (0, 2), (1, 1), (1, 0), (0, 1), (0, 0)]
ALPHA = 2.0


def stack_constants():
    place = np.zeros((P, 2, PARTS, P), np.float32)
    for q, (w_part, a_part) in enumerate(PRODUCTS):
        for r in range(RANK):
            place[r::RANK, 0, a_part, RANK * q + r] = 1.0
            place[r::RANK, 1, w_part, RANK * q + r] = 1.0
    return place.reshape(P, 2, PARTS * P)


def small_constants():
    small = np.zeros((P, 1 + EXPERTS), np.float32)
    small[:, 0] = np.arange(P)
    for e in range(EXPERTS):
        small[RANK * e:RANK * (e + 1), 1 + e] = 1.0
    return small


def cond_resid_kernel(nc, x, experts, delta_t, cats, w0, b0, amplitudes, frequencies, w2, b2, wi, wo,
                      common_wi_a, common_wi_b, common_wo_a, common_wo_b,
                      experts_wi_a, experts_wi_b, experts_wo_a, experts_wo_b,
                      identity, place, small, out):
    x_rows = x.rearrange("b s d -> (b s) d").rearrange("(q t p) d -> q p t d", t=TILES, p=P)
    out_rows = out.rearrange("b s d -> (b s) d").rearrange("(q t p) d -> q p t d", t=TILES, p=P)
    rotation_dram = nc.dram_tensor("rotation_scratch", (2, BATCH * SEQ), FP32, kind="Internal").ap()

    ctx = ExitStack()
    with ctx:
        def sb(name, shape, dtype=FP32, stack=ctx):
            return stack.enter_context(nc.sbuf_tensor(name, shape, dtype))

        def sem(name):
            return ctx.enter_context(nc.semaphore(name))

        ident = sb("ident", [P, P])
        small_sb = sb("small_sb", [P, 1 + EXPERTS])
        wi_hi, wi_lo = (sb(f"wi_{n}", [P, HALVES, F], F32R) for n in ("hi", "lo"))
        wo_hi, wo_lo = (sb(f"wo_{n}", [P, FT, D], F32R) for n in ("hi", "lo"))
        ia_hi, ia_lo = (sb(f"ia_{n}", [P, HALVES, P], F32R) for n in ("hi", "lo"))
        oa_hi, oa_lo = (sb(f"oa_{n}", [P, FT, P], F32R) for n in ("hi", "lo"))
        w0_parts = sb("w0_parts", [P, EXPERTS, PARTS, HALVES * D], BF16)
        ib_stack = sb("ib_stack", [P, EXPERTS, F], BF16)
        ob_stack = sb("ob_stack", [P, EXPERTS, D], BF16)
        pick = sb("pick", [P, EXPERTS, PARTS * P], BF16)
        bias = sb("bias", [P, 2 * HALVES, BATCH])
        index_given = sb("index_given", [1, 2, BATCH], I32)
        index = sb("index", [1, 2, BATCH], I32)

        x_sb = sb("x_sb", [P, TILES, D])
        rotation = sb("rotation", [P, 2, GT])
        w2_raw = sb("w2_raw", [P, SPG, HALVES * D])
        hid_hi, hid_lo = (sb(f"hid_{n}", [P, FT, GT], F32R) for n in ("hi", "lo"))
        y2_hi, y2_lo = (sb(f"y2_{n}", [P, HALVES, GT], F32R) for n in ("hi", "lo"))
        out_sb = sb("out_sb", [P, TILES, D])

        scratch = ExitStack()
        wi_nat = sb("wi_nat", [P, FT, D], FP32, scratch)
        wo_nat = sb("wo_nat", [P, HALVES, F], FP32, scratch)
        w0_nat = sb("w0_nat", [P, 2, HALVES, D], FP32, scratch)
        ia_nat = sb("ia_nat", [P, D], FP32, scratch)
        ib_nat = sb("ib_nat", [P, FT, P], FP32, scratch)
        oa_nat = sb("oa_nat", [P, F], FP32, scratch)
        ob_nat = sb("ob_nat", [P, HALVES, P], FP32, scratch)
        cia = sb("cia", [RANK, D], FP32, scratch)
        cib_nat = sb("cib_nat", [P, FT, RANK], FP32, scratch)
        coa = sb("coa", [RANK, F], FP32, scratch)
        cob_nat = sb("cob_nat", [P, HALVES, RANK], FP32, scratch)
        cia2 = sb("cia2", [RANK, D], FP32, scratch)
        coa2 = sb("coa2", [RANK, F], FP32, scratch)
        cib_t = sb("cib_t", [RANK, F], FP32, scratch)
        cob_t = sb("cob_t", [RANK, D], FP32, scratch)
        place_sb = sb("place_sb", [P, 2, PARTS * P], FP32, scratch)
        put = sb("put", [P, EXPERTS, PARTS * P], BF16, scratch)
        ib_parts = sb("ib_parts", [P, PARTS, F], BF16, scratch)
        ob_parts = sb("ob_parts", [P, PARTS, D], BF16, scratch)
        rest = sb("rest", [P, 2, 512], FP32, scratch)
        b0_nat = sb("b0_nat", [EXPERTS, D], FP32, scratch)
        b2_nat = sb("b2_nat", [CATEGORIES, D], FP32, scratch)
        index_all = sb("index_all", [CATEGORIES, 2, BATCH], I32, scratch)
        index_f = sb("index_f", [CATEGORIES, 2, BATCH], FP32, scratch)
        one_hot = sb("one_hot", [CATEGORIES, 2, BATCH], FP32, scratch)
        rot = sb("rot", [P, 14, SEQ], FP32, scratch)
        dt_sb = sb("dt_sb", [P, 1], FP32, scratch)
        scratch.close()

        w0_stage = sb("w0_stage", [P, SPG, PARTS, HALVES * D], BF16)
        ib_stage = sb("ib_stage", [P, SPG, F], BF16)
        ob_stage = sb("ob_stage", [P, SPG, D], BF16)
        pick_stage = sb("pick_stage", [P, SPG, PARTS * P], BF16)
        w2_parts = sb("w2_parts", [P, SPG, PARTS, HALVES * D], BF16)
        x_parts = sb("x_parts", [P, PARTS, HALVES, GT], BF16)
        x_rest = sb("x_rest", [P, HALVES, GT])
        x_bias = sb("x_bias", [P, HALVES, GT])
        y0 = sb("y0", [P, HALVES, GT])
        y0_cos = sb("y0_cos", [P, HALVES, GT])
        y0_sin = sb("y0_sin", [P, HALVES, GT])
        y1 = sb("y1", [P, HALVES, GT])
        y1_rest = sb("y1_rest", [P, HALVES, GT])
        y1_parts = sb("y1_parts", [P, PARTS, HALVES, GT], BF16)
        y1_bias = sb("y1_bias", [P, HALVES, GT])
        y2 = sb("y2", [P, 2, HALVES, GT])
        low_parts = sb("low_parts", [P, PARTS, GT], BF16)
        low_rest = sb("low_rest", [P, GT])
        stack = sb("stack", [P, GT], BF16)
        y3 = sb("y3", [P, HALVES, GT])

        banks = [ctx.enter_context(nc.psum_tensor(f"bank{n}", [P, 512], FP32)) for n in range(8)]

        def halves(bank):
            return bank[:, :].rearrange("p (h t) -> p h t", h=HALVES)

        turn_bank = banks[0]
        front_bank = banks[1]
        hidden_banks = banks[2:6]
        out_bank = banks[6]
        low_bank = banks[7][:, 0:GT]
        stack_bank = banks[7][:, GT:2 * GT]

        in_ident = sem("in_ident")
        in_index = sem("in_index")
        index_ready = sem("index_ready")
        in_rot = sem("in_rot")
        in_lora_a = sem("in_lora_a")
        in_lora_b = sem("in_lora_b")
        in_common = sem("in_common")
        in_wi = sem("in_wi")
        in_wo = sem("in_wo")
        in_bias = sem("in_bias")
        in_w0 = [sem("in_w0_0"), sem("in_w0_1")]
        rot_step = sem("rot_step")
        rot_angles = sem("rot_angles")
        rot_power = sem("rot_power")
        rot_trig = sem("rot_trig")
        rot_saved = sem("rot_saved")
        pick_done = sem("pick_done")
        hot_step = sem("hot_step")
        hot_done = sem("hot_done")
        common_scaled = sem("common_scaled")
        pre_full = sem("pre_full")
        pre_high = sem("pre_high")
        pre_rest = sem("pre_rest")
        pre_low = sem("pre_low")
        pre_step = sem("pre_step")
        exp_full = sem("exp_full")
        exp_w0_full = sem("exp_w0_full")
        exp_w0_high = sem("exp_w0_high")
        exp_w0_rest = sem("exp_w0_rest")
        exp_w0_mid = sem("exp_w0_mid")
        exp_w0_low = sem("exp_w0_low")
        exp_act = sem("exp_act")
        exp_dve = sem("exp_dve")
        pre_pe_done = sem("pre_pe_done")

        x_in = sem("x_in")
        rotation_in = sem("rotation_in")
        w2_in = [sem(f"w2_in{s}") for s in range(SPG)]
        out_stored = sem("out_stored")
        x_turned = sem("x_turned")
        l0_full = sem("l0_full")
        l2_full = sem("l2_full")
        low1_full = sem("low1_full")
        low2_full = sem("low2_full")
        stack1_full = sem("stack1_full")
        stack2_full = sem("stack2_full")
        hidden_full = [sem(f"hidden_full{k}") for k in range(PAIRS)]
        out_full = sem("out_full")
        out_turned = sem("out_turned")
        x_high = sem("x_high")
        x_rested = sem("x_rested")
        x_biased = sem("x_biased")
        x_mid = sem("x_mid")
        x_split = sem("x_split")
        y0_done = sem("y0_done")
        y0_cos_done = sem("y0_cos_done")
        y0_sin_done = sem("y0_sin_done")
        y1_done = sem("y1_done")
        y1_high = sem("y1_high")
        y1_rested = sem("y1_rested")
        y1_mid = sem("y1_mid")
        y1_split = sem("y1_split")
        y1_biased = sem("y1_biased")
        y2_done = sem("y2_done")
        y2_high = sem("y2_high")
        y2_split = sem("y2_split")
        low1_high, low1_rested, low1_mid, low1_split = (sem(f"low1_{n}") for n in ("high", "rested", "mid", "split"))
        low2_high, low2_rested, low2_mid, low2_split = (sem(f"low2_{n}") for n in ("high", "rested", "mid", "split"))
        stack1_done = sem("stack1_done")
        stack2_done = sem("stack2_done")
        hid_high = [sem(f"hid_high{k}") for k in range(PAIRS)]
        hid_split = [sem(f"hid_split{k}") for k in range(PAIRS)]
        y3_done = sem("y3_done")
        out_taken = sem("out_taken")
        w2_high = [sem(f"w2_high{s}") for s in range(SPG)]
        w2_rested = [sem(f"w2_rested{s}") for s in range(SPG)]
        w2_mid = [sem(f"w2_mid{s}") for s in range(SPG)]
        w2_split = [sem(f"w2_split{s}") for s in range(SPG)]
        w0_staged = sem("w0_staged")
        ib_staged = sem("ib_staged")
        ob_staged = sem("ob_staged")
        pick_staged = sem("pick_staged")

        SPLIT2, SPLIT3, COPY = "two float32r parts", "three bfloat16 parts", "a copy"
        JOBS = []
        JOBS.append((SPLIT2, "ia", 0))
        JOBS += [(SPLIT2, "oa", n) for n in range(2)]
        JOBS += [(SPLIT3, "ib", n) for n in range(2)]
        JOBS.append((SPLIT3, "ob", 0))
        JOBS += [(COPY, "cib", n) for n in range(2)]
        JOBS.append((COPY, "cob", 0))
        JOBS.append((COPY, "bias", 0))
        JOBS += [(SPLIT2, "wi", n) for n in range(4)]
        JOBS += [(SPLIT2, "wo", n) for n in range(FT // 2)]
        HIGHS = [j + 1 for j in range(len(JOBS))]
        RESTS = [sum(JOBS[i][0] != COPY for i in range(j + 1)) for j in range(len(JOBS))]

        def job_views(j):
            how, name, n = JOBS[j]
            bank = banks[j % 8]
            if name == "ia":
                return bank[:, 0:256].rearrange("p (h e) -> p h e", h=HALVES), (ia_hi[:], ia_lo[:])
            if name == "oa":
                t = slice(4 * n, 4 * n + 4)
                return bank[:, :].rearrange("p (k e) -> p k e", k=4), (oa_hi[:, t, :], oa_lo[:, t, :])
            if name == "ib":
                return bank[:, :], [ib_parts[:, q, 512 * n:512 * (n + 1)] for q in range(PARTS)]
            if name == "ob":
                return bank[:, 0:D], [ob_parts[:, q, :] for q in range(PARTS)]
            if name == "cib":
                return bank[0:RANK, :], (cib_t[:, 512 * n:512 * (n + 1)],)
            if name == "cob":
                return bank[0:RANK, 0:D], (cob_t[:, :],)
            if name == "bias":
                return bank[:, :].rearrange("p (h b) -> p h b", h=2 * HALVES), (bias[:],)
            if name == "wi":
                k, c = n // 2, slice(512 * (n % 2), 512 * (n % 2) + 512)
                return bank[:, :], (wi_hi[:, k, c], wi_lo[:, k, c])
            if name == "wo":
                t = slice(2 * n, 2 * n + 2)
                return bank[:, :].rearrange("p (k d) -> p k d", k=2), (wo_hi[:, t, :], wo_lo[:, t, :])

        SP, SCALAR, VECTOR = mybir.EngineType.SP, mybir.EngineType.Activation, mybir.EngineType.DVE

        def group_indices(engine, which, q):
            _, values = nc.values_load_multi_w_load_instructions(
                index[0:1, which, bass.ds(SPG * q, SPG)], engines=(engine,), min_val=0,
                max_val=(EXPERTS, CATEGORIES)[which] - 1,
                skip_runtime_bounds_check_because="VectorE clamped the indices to this range")
            return values

        block = ctx.enter_context(nc.Block())

        @block.sync
        def _(sp):
            sp.dma_start(index_given[:, 0, :], experts.rearrange("(o b) -> o b", o=1)).then_inc(in_index, 16)
            sp.dma_start(index_given[:, 1, :], cats.rearrange("(o b) -> o b", o=1)).then_inc(in_index, 16)
            sp.dma_start(dt_sb[:], delta_t.rearrange("(b o) -> b o", o=1)).then_inc(in_rot, 16)
            sp.dma_start(rot[:, 0, :], amplitudes.partition_broadcast(P)).then_inc(in_rot, 16)
            sp.dma_start(rot[:, 1, :], frequencies.partition_broadcast(P)).then_inc(in_rot, 16)
            sp.dma_start(ident[:], identity).then_inc(in_ident, 16)
            sp.dma_start(ia_nat[:], experts_wi_a.rearrange("e r d -> (e r) d")).then_inc(in_lora_a, 16)
            sp.dma_start(oa_nat[:], experts_wo_a.rearrange("e r f -> (e r) f")).then_inc(in_lora_a, 16)
            for e in range(EXPERTS):
                columns = slice(RANK * e, RANK * (e + 1))
                sp.dma_start(ib_nat[:, :, columns],
                             experts_wi_b[e].rearrange("(t p) r -> p t r", p=P)).then_inc(in_lora_b, 16)
                sp.dma_start(ob_nat[:, :, columns],
                             experts_wo_b[e].rearrange("(t p) r -> p t r", p=P)).then_inc(in_lora_b, 16)
            sp.dma_start(x_sb[:], x_rows[0]).then_inc(x_in, 16)

            def load_w2(q, s, category):
                sp.dma_start(w2_raw[:, s, :].rearrange("p (h d) -> p h d", h=HALVES),
                             w2[bass.ds(category, 1)].rearrange("o (h p) d -> p (o h) d", p=P)
                             ).then_inc(w2_in[s], 16)

            def load_rotation(q):
                sp.dma_start(rotation[:], rotation_dram[:, bass.ds(GT * q, GT)].partition_broadcast(P)
                             ).then_inc(rotation_in, 16)

            sp.wait_ge(index_ready, 1)
            categories = group_indices(SP, 1, 0)
            for s in range(SPG):
                load_w2(0, s, categories[s])
            sp.wait_ge(rot_trig, 1)
            sp.dma_start(rotation_dram[0].rearrange("(b s) -> b s", s=SEQ), rot[:, 12, :]).then_inc(rot_saved, 16)
            sp.dma_start(rotation_dram[1].rearrange("(b s) -> b s", s=SEQ), rot[:, 13, :]).then_inc(rot_saved, 16)
            sp.wait_ge(rot_saved, 32)
            load_rotation(0)

            def load_x(q):
                sp.wait_ge(x_turned, q)
                sp.dma_start(x_sb[:], x_rows[bass.ds(q, 1)].rearrange("o p t d -> p (o t) d")).then_inc(x_in, 16)

            def load_categories(q):
                categories = group_indices(SP, 1, q)
                for s in range(SPG):
                    sp.wait_ge(w2_split[s], q)
                    load_w2(q, s, categories[s])

            def load_factors(q):
                sp.wait_ge(y0_sin_done, q)
                load_rotation(q)

            def store(g):
                sp.wait_ge(out_taken, g + 2)
                sp.dma_start(out_rows[bass.ds(g, 1)].rearrange("o p t d -> p (o t) d"), out_sb[:]
                             ).then_inc(out_stored, 16)

            load_x(1)
            load_factors(1)
            load_categories(1)
            load_x(2)
            load_factors(2)
            with sp.Fori(0, GROUPS - 3) as g:
                load_x(g + 3)
                load_categories(g + 2)
                load_factors(g + 3)
                store(g)
            load_categories(GROUPS - 1)
            for g in range(GROUPS - 3, GROUPS):
                store(g)
            sp.wait_ge(out_stored, 16 * (GROUPS + 1))

        @block.gpsimd
        def _(pool):
            pool.wait_ge(in_rot, 48)
            nc.gpsimd.tensor_tensor(rot[:, 2, :], rot[:, 0, :], dt_sb[:, 0:1].to_broadcast([P, SEQ]),
                                    ALU.pow).then_inc(rot_power, 1)

            def w2_take_high(q):
                for s in range(SPG):
                    pool.wait_ge(w2_high[s], q + 1)
                    nc.gpsimd.tensor_tensor(w2_raw[:, s, :], w2_raw[:, s, :], w2_parts[:, s, 0, :],
                                            ALU.subtract).then_inc(w2_rested[s], 1)

            def w2_take_mid(q):
                for s in range(SPG):
                    pool.wait_ge(w2_mid[s], q + 1)
                    nc.gpsimd.tensor_tensor(w2_parts[:, s, 2, :], w2_raw[:, s, :], w2_parts[:, s, 1, :],
                                            ALU.subtract).then_inc(w2_split[s], 1)

            def add_bias2(q):
                pool.wait_ge(y1_done, q + 1)
                b = bias[:, HALVES:2 * HALVES, bass.ds(SPG * q, SPG)].unsqueeze(3)
                nc.gpsimd.tensor_tensor(y1_bias[:].rearrange("p h (s t) -> p h s t", s=SPG),
                                        y1[:].rearrange("p h (s t) -> p h s t", s=SPG),
                                        b.to_broadcast([P, HALVES, SPG, SEQ]), ALU.add).then_inc(y1_biased, 1)

            w2_take_high(0)
            w2_take_mid(0)
            add_bias2(0)
            w2_take_high(1)
            w2_take_mid(1)
            add_bias2(1)
            with pool.Fori(0, GROUPS - 2) as g:
                w2_take_high(g + 2)
                w2_take_mid(g + 2)
                add_bias2(g + 2)

        @block.scalar
        def _(act):
            act.dma_start(small_sb[:], small).then_inc(in_bias, 16)
            act.dma_start(index_all[:, 0, :], experts.partition_broadcast(CATEGORIES)).then_inc(in_bias, 16)
            act.dma_start(index_all[:, 1, :], cats.partition_broadcast(CATEGORIES)).then_inc(in_bias, 16)
            act.dma_start(b0_nat[:], b0).then_inc(in_bias, 16)
            act.dma_start(b2_nat[:], b2).then_inc(in_bias, 16)
            act.dma_start(place_sb[:], place).then_inc(in_bias, 16)
            act.dma_start(cia[:], common_wi_a).then_inc(in_common, 16)
            act.dma_start(coa[:], common_wo_a).then_inc(in_common, 16)
            act.dma_start(cib_nat[:], common_wi_b.rearrange("(t p) r -> p t r", p=P)).then_inc(in_common, 16)
            act.dma_start(cob_nat[:], common_wo_b.rearrange("(t p) r -> p t r", p=P)).then_inc(in_common, 16)
            act.dma_start(wi_nat[:], wi.rearrange("(t p) d -> p t d", p=P)).then_inc(in_wi, 16)
            act.dma_start(wo_nat[:], wo.rearrange("(t p) f -> p t f", p=P)).then_inc(in_wo, 16)

            def load_w0(e, slot):
                act.dma_start(w0_nat[:, slot], w0[bass.ds(e, 1)].rearrange("o (h p) d -> p (o h) d", p=P)
                              ).then_inc(in_w0[slot], 16)

            load_w0(0, 0)
            load_w0(1, 1)
            act.wait_ge(rot_angles, 1)
            nc.scalar.activation(rot[:, 10, :], rot[:, 8, :], ACT.Sin)
            nc.scalar.activation(rot[:, 11, :], rot[:, 9, :], ACT.Sin).then_inc(rot_step, 100)
            act.wait_ge(in_common, 64)
            nc.scalar.mul(cia2[:], cia[:], ALPHA)
            nc.scalar.mul(coa2[:], coa[:], ALPHA).then_inc(common_scaled, 1)

            for j, (how, name, n) in enumerate(JOBS):
                bank, parts = job_views(j)
                act.wait_ge(pre_full, j + 1)
                nc.scalar.copy(parts[0], bank).then_inc(pre_high, 1)

            def two_experts(t, more):
                act.wait_ge(exp_w0_full, t + 1)
                if more:
                    for i in range(2):
                        load_w0(2 * t + 2 + i, i)
                for i in range(2):
                    nc.scalar.copy(w0_parts[:, bass.ds(2 * t + i, 1), 0, :].rearrange("p o c -> p (o c)"),
                                   banks[i][:, :]).then_inc(exp_w0_high, 1)
                for i in range(2):
                    act.wait_ge(exp_w0_rest, 2 * t + i + 1)
                    nc.scalar.copy(w0_parts[:, bass.ds(2 * t + i, 1), 1, :].rearrange("p o c -> p (o c)"),
                                   rest[:, i, :]).then_inc(exp_w0_mid, 1)
                act.wait_ge(exp_full, t + 1)
                for i in range(2):
                    nc.scalar.copy(ib_stack[:, bass.ds(2 * t + i, 1), 0:512].rearrange("p o c -> p (o c)"),
                                   banks[2 + 2 * i][:, :])
                nc.scalar.copy(ob_stack[:, bass.ds(2 * t, 2), :].rearrange("p o c -> p (o c)"),
                               banks[6][:, :]).then_inc(exp_act, 1)

            with act.Fori(0, EXPERTS // 2 - 1) as t:
                two_experts(t, True)
            two_experts(EXPERTS // 2 - 1, False)

            def x_take_high(q):
                act.wait_ge(x_turned, q + 1)
                nc.scalar.copy(x_parts[:, 0], halves(turn_bank)).then_inc(x_high, 1)

            def x_take_mid(q):
                act.wait_ge(x_rested, q + 1)
                nc.scalar.copy(x_parts[:, 1], x_rest[:]).then_inc(x_mid, 1)

            def y1_take_high(q):
                act.wait_ge(y1_done, q + 1)
                nc.scalar.copy(y1_parts[:, 0], y1[:]).then_inc(y1_high, 1)

            def y1_take_mid(q):
                act.wait_ge(y1_rested, q + 1)
                nc.scalar.copy(y1_parts[:, 1], y1_rest[:]).then_inc(y1_mid, 1)

            def y2_take_high(q):
                act.wait_ge(y2_done, q + 1)
                nc.scalar.copy(y2_hi[:], y2[:, bass.ds(q % 2, 1)].rearrange("p o h t -> p (o h) t")
                               ).then_inc(y2_high, 1)

            def low_take_high(q, full, high):
                act.wait_ge(full, q + 1)
                nc.scalar.copy(low_parts[:, 0], low_bank).then_inc(high, 1)

            def low_take_mid(q, rested, mid):
                act.wait_ge(rested, q + 1)
                nc.scalar.copy(low_parts[:, 1], low_rest[:]).then_inc(mid, 1)

            def take_stack(q, full, done):
                act.wait_ge(full, q + 1)
                nc.scalar.copy(stack[:], stack_bank).then_inc(done, 1)

            def hidden_take_high(g, k):
                act.wait_ge(hidden_full[k], g + 1)
                nc.scalar.activation(hid_hi[:, 2 * k:2 * k + 2, :], halves(hidden_banks[k]), ACT.Relu
                                     ).then_inc(hid_high[k], 1)

            def w2_take_high(q, samples=range(SPG)):
                for s in samples:
                    act.wait_ge(w2_in[s], 16 * q + 16)
                    nc.scalar.copy(w2_parts[:, s, 0, :], w2_raw[:, s, :]).then_inc(w2_high[s], 1)

            def w2_take_mid(q):
                for s in range(SPG):
                    act.wait_ge(w2_rested[s], q + 1)
                    nc.scalar.copy(w2_parts[:, s, 1, :], w2_raw[:, s, :]).then_inc(w2_mid[s], 1)

            def take_out(g):
                act.wait_ge(out_turned, g + 1)
                act.wait_ge(out_stored, 16 * g + 16)
                nc.scalar.copy(out_sb[:], turn_bank[:, :].rearrange("p (t d) -> p t d", t=TILES)
                               ).then_inc(out_taken, 1)

            def stage_ib(q):
                experts_of = group_indices(SCALAR, 0, q)
                for s in range(SPG):
                    last = nc.scalar.copy(ib_stage[:, s, :],
                                          ib_stack[:, bass.ds(experts_of[s], 1), :].rearrange("p o c -> p (o c)"))
                last.then_inc(ib_staged, 1)

            def body(g, middle, front):
                n, m = g + 1, g + 2
                if front:
                    x_take_high(m)
                hidden_take_high(g, 0)
                hidden_take_high(g, 1)
                if front:
                    x_take_mid(m)
                hidden_take_high(g, 2)
                hidden_take_high(g, 3)
                if middle:
                    stage_ib(n)
                    y2_take_high(n)
                low_take_high(g, low2_full, low2_high)
                if front:
                    w2_take_high(n + 1, [0])
                low_take_mid(g, low2_rested, low2_mid)
                if front:
                    w2_take_high(n + 1, [1, 2, 3])
                take_stack(g, stack2_full, stack2_done)
                if front:
                    w2_take_mid(n + 1)
                    y1_take_high(m)
                if middle:
                    low_take_high(n, low1_full, low1_high)
                    low_take_mid(n, low1_rested, low1_mid)
                if front:
                    y1_take_mid(m)
                take_out(g)
                if middle:
                    take_stack(n, stack1_full, stack1_done)

            act.wait_ge(pre_pe_done, 1)
            act.wait_ge(exp_dve, EXPERTS // 2)
            act.wait_ge(index_ready, 1)
            act.sem_inc(out_taken, 1)
            act.sem_inc(out_stored, 16)
            w2_take_high(0)
            x_take_high(0)
            x_take_mid(0)
            w2_take_mid(0)
            y1_take_high(0)
            y1_take_mid(0)
            stage_ib(0)
            x_take_high(1)
            x_take_mid(1)
            y2_take_high(0)
            w2_take_high(1)
            w2_take_mid(1)
            y1_take_high(1)
            y1_take_mid(1)
            low_take_high(0, low1_full, low1_high)
            low_take_mid(0, low1_rested, low1_mid)
            take_stack(0, stack1_full, stack1_done)
            with act.Fori(0, GROUPS - 2) as g:
                body(g, True, True)
            body(GROUPS - 2, True, False)
            body(GROUPS - 1, False, False)

        @block.vector
        def _(dve):
            steps = [0]

            def then(instruction):
                steps[0] += 1
                instruction.then_inc(pre_step, 1)
                dve.wait_ge(pre_step, steps[0])

            TWO_PI = 2.0 * np.pi
            ROUND = 1.5 * 2.0 ** 23
            C1 = 6.28125
            C2 = float(np.float32(np.round((TWO_PI - C1) * 2.0 ** 21) / 2.0 ** 21))
            C3 = float(np.float32(TWO_PI - C1 - C2))
            LIMIT = 3.1415925
            dve.wait_ge(in_index, 32)
            nc.vector.tensor_scalar(index[:, 0, :], index_given[:, 0, :], 0, EXPERTS - 1, ALU.max, ALU.min)
            nc.vector.tensor_scalar(index[:, 1, :], index_given[:, 1, :], 0, CATEGORIES - 1, ALU.max, ALU.min
                                    ).then_inc(index_ready, 1)
            dve.wait_ge(in_rot, 48)
            then(nc.vector.tensor_scalar(rot[:, 3, :], rot[:, 1, :], dt_sb[:, 0:1], None, ALU.mult))
            for at, offset, shift in ((4, 0.0, 0.0), (5, 0.25, 0.5 * np.pi)):
                angle = 8 if at == 4 else 9
                then(nc.vector.tensor_scalar(rot[:, at, :], rot[:, 3, :], float(1.0 / TWO_PI), offset, ALU.mult, ALU.add))
                then(nc.vector.tensor_scalar(rot[:, 6, :], rot[:, at, :], ROUND, None, ALU.add))
                then(nc.vector.tensor_scalar(rot[:, 7, :], rot[:, 6, :], -ROUND, None, ALU.add))
                then(nc.vector.scalar_tensor_tensor(rot[:, at, :], rot[:, 7, :], -C1, rot[:, 3, :], ALU.mult, ALU.add))
                then(nc.vector.scalar_tensor_tensor(rot[:, 6, :], rot[:, 7, :], -C2, rot[:, at, :], ALU.mult, ALU.add))
                then(nc.vector.scalar_tensor_tensor(rot[:, at, :], rot[:, 7, :], -C3, rot[:, 6, :], ALU.mult, ALU.add))
                then(nc.vector.tensor_scalar(rot[:, 6, :], rot[:, at, :], shift, LIMIT, ALU.add, ALU.min))
                then(nc.vector.tensor_scalar(rot[:, angle, :], rot[:, 6, :], -LIMIT, None, ALU.max))
            nc.vector.memset(rot[0:1, 7, 0:1], 0.0).then_inc(rot_angles, 1)
            dve.wait_ge(in_bias, 96)
            then(nc.vector.tensor_copy(index_f[:], index_all[:]))
            nc.vector.tensor_scalar(one_hot[:], index_f[:], small_sb[0:CATEGORIES, 0:1], None, ALU.is_equal).then_inc(hot_done, 1)
            for e in range(EXPERTS):
                nc.vector.tensor_scalar(pick[:, e, :], place_sb[:, 0, :], small_sb[:, 1 + e:2 + e], ALPHA, ALU.mult, ALU.mult)
                last = nc.vector.tensor_scalar(put[:, e, :], place_sb[:, 1, :], small_sb[:, 1 + e:2 + e], None, ALU.mult)
            last.then_inc(pick_done, 1)
            dve.wait_ge(rot_power, 1)
            dve.wait_ge(rot_step, 100)
            then(nc.vector.tensor_tensor(rot[:, 4, :], rot[:, 2, :], rot[:, 11, :], ALU.mult))
            nc.vector.tensor_scalar(rot[:, 12, :], rot[:, 4, :], 1.0, None, ALU.add)
            nc.vector.tensor_tensor(rot[:, 13, :], rot[:, 2, :], rot[:, 10, :], ALU.mult).then_inc(rot_trig, 1)

            rests = 0
            for j, (how, name, n) in enumerate(JOBS):
                if how == COPY:
                    continue
                bank, parts = job_views(j)
                dve.wait_ge(pre_high, HIGHS[j])
                if how == SPLIT2:
                    nc.vector.tensor_tensor(parts[1], bank, parts[0], ALU.subtract).then_inc(pre_rest, 1)
                    rests += 1
                else:
                    width = 512 if name == "ib" else D
                    room = rest[:, 0, 0:width]
                    nc.vector.tensor_tensor(room, bank, parts[0], ALU.subtract).then_inc(pre_rest, 1)
                    rests += 1
                    dve.wait_ge(pre_rest, rests)
                    then(nc.vector.tensor_copy(parts[1], room))
                    then(nc.vector.tensor_tensor(parts[2], room, parts[1], ALU.subtract))
            nc.vector.memset(rest[0:1, 1, 0:1], 0.0).then_inc(pre_low, 1)

            with dve.Fori(0, EXPERTS // 2) as t:
                for i in range(2):
                    dve.wait_ge(exp_w0_high, 2 * t + i + 1)
                    nc.vector.tensor_tensor(rest[:, i, :], banks[i][:, :],
                                            w0_parts[:, bass.ds(2 * t + i, 1), 0, :].rearrange("p o c -> p (o c)"),
                                            ALU.subtract).then_inc(exp_w0_rest, 1)
                for i in range(2):
                    dve.wait_ge(exp_w0_mid, 2 * t + i + 1)
                    nc.vector.tensor_tensor(w0_parts[:, bass.ds(2 * t + i, 1), 2, :].rearrange("p o c -> p (o c)"),
                                            rest[:, i, :],
                                            w0_parts[:, bass.ds(2 * t + i, 1), 1, :].rearrange("p o c -> p (o c)"),
                                            ALU.subtract).then_inc(exp_w0_low, 1)
                dve.wait_ge(exp_full, t + 1)
                dve.wait_ge(exp_w0_low, 2 * t + 2)
                for i in range(2):
                    last = nc.vector.tensor_copy(ib_stack[:, bass.ds(2 * t + i, 1), 512:1024].rearrange("p o c -> p (o c)"),
                                                 banks[3 + 2 * i][:, :])
                last.then_inc(exp_dve, 1)

            def stage_w0(experts_of):
                for s in range(SPG):
                    last = nc.vector.tensor_copy(w0_stage[:, s].rearrange("p k c -> p (k c)"),
                                                 w0_parts[:, bass.ds(experts_of[s], 1)].rearrange("p o k c -> p (o k c)"))
                last.then_inc(w0_staged, 1)

            def stage_ob(experts_of):
                for s in range(SPG):
                    last = nc.vector.tensor_copy(ob_stage[:, s, :],
                                                 ob_stack[:, bass.ds(experts_of[s], 1), :].rearrange("p o c -> p (o c)"))
                last.then_inc(ob_staged, 1)

            def stage_pick(experts_of):
                for s in range(SPG):
                    last = nc.vector.tensor_copy(pick_stage[:, s, :],
                                                 pick[:, bass.ds(experts_of[s], 1), :].rearrange("p o c -> p (o c)"))
                last.then_inc(pick_staged, 1)

            def x_take_rest(q):
                dve.wait_ge(x_high, q + 1)
                nc.vector.tensor_tensor(x_rest[:], halves(turn_bank), x_parts[:, 0], ALU.subtract).then_inc(x_rested, 1)

            def x_add_bias(q):
                b = bias[:, 0:HALVES, bass.ds(SPG * q, SPG)].unsqueeze(3)
                nc.vector.tensor_tensor(x_bias[:].rearrange("p h (s t) -> p h s t", s=SPG),
                                        turn_bank[:, :].rearrange("p (h s t) -> p h s t", h=HALVES, s=SPG),
                                        b.to_broadcast([P, HALVES, SPG, SEQ]), ALU.add).then_inc(x_biased, 1)

            def x_take_low(q):
                dve.wait_ge(x_mid, q + 1)
                nc.vector.tensor_tensor(x_parts[:, 2], x_rest[:], x_parts[:, 1], ALU.subtract).then_inc(x_split, 1)

            def hidden_take_low(g, k):
                dve.wait_ge(hid_high[k], g + 1)
                nc.vector.scalar_tensor_tensor(hid_lo[:, 2 * k:2 * k + 2, :], halves(hidden_banks[k]), 0.0,
                                               hid_hi[:, 2 * k:2 * k + 2, :], ALU.max, ALU.subtract
                                               ).then_inc(hid_split[k], 1)

            def l0_sum(q):
                dve.wait_ge(l0_full, q + 1)
                dve.wait_ge(x_biased, q + 1)
                nc.vector.tensor_tensor(y0[:], halves(front_bank), x_bias[:], ALU.add).then_inc(y0_done, 1)

            def rotate(q):
                dve.wait_ge(rotation_in, 16 * q + 16)
                dve.wait_ge(y0_done, q + 1)
                nc.vector.tensor_tensor(y0_cos[:], y0[:], rotation[:, 0, :].unsqueeze(1).to_broadcast([P, HALVES, GT]),
                                        ALU.mult).then_inc(y0_cos_done, 1)
                nc.vector.tensor_tensor(y0_sin[:], y0[:], rotation[:, 1, :].unsqueeze(1).to_broadcast([P, HALVES, GT]),
                                        ALU.mult).then_inc(y0_sin_done, 1)

            def rotate_sum(q):
                dve.wait_ge(y0_cos_done, q + 1)
                dve.wait_ge(y0_sin_done, q + 1)
                nc.vector.tensor_tensor(y1[:, 0], y0_cos[:, 0], y0_sin[:, 1], ALU.subtract)
                nc.vector.tensor_tensor(y1[:, 1], y0_sin[:, 0], y0_cos[:, 1], ALU.add).then_inc(y1_done, 1)

            def y1_take_rest(q):
                dve.wait_ge(y1_high, q + 1)
                nc.vector.tensor_tensor(y1_rest[:], y1[:], y1_parts[:, 0], ALU.subtract).then_inc(y1_rested, 1)

            def y1_take_low(q):
                dve.wait_ge(y1_mid, q + 1)
                nc.vector.tensor_tensor(y1_parts[:, 2], y1_rest[:], y1_parts[:, 1], ALU.subtract).then_inc(y1_split, 1)

            def low_take_rest(q, high, rested):
                dve.wait_ge(high, q + 1)
                nc.vector.tensor_tensor(low_rest[:], low_bank, low_parts[:, 0], ALU.subtract).then_inc(rested, 1)

            def low_take_low(q, mid, split):
                dve.wait_ge(mid, q + 1)
                nc.vector.tensor_tensor(low_parts[:, 2], low_rest[:], low_parts[:, 1], ALU.subtract).then_inc(split, 1)

            def l2_sum(q):
                dve.wait_ge(l2_full, q + 1)
                dve.wait_ge(y1_biased, q + 1)
                nc.vector.tensor_tensor(y2[:, bass.ds(q % 2, 1)].rearrange("p o h t -> p (o h) t"),
                                        halves(front_bank), y1_bias[:], ALU.add).then_inc(y2_done, 1)

            def y2_take_low(q):
                dve.wait_ge(y2_high, q + 1)
                nc.vector.tensor_tensor(y2_lo[:], y2[:, bass.ds(q % 2, 1)].rearrange("p o h t -> p (o h) t"),
                                        y2_hi[:], ALU.subtract).then_inc(y2_split, 1)

            def l3_sum(g):
                dve.wait_ge(out_full, g + 1)
                nc.vector.tensor_tensor(y3[:], halves(out_bank),
                                        y2[:, bass.ds(g % 2, 1)].rearrange("p o h t -> p (o h) t"),
                                        ALU.add).then_inc(y3_done, 1)

            def body(g, middle, front):
                n, m = g + 1, g + 2
                if front:
                    x_take_rest(m)
                hidden_take_low(g, 0)
                hidden_take_low(g, 1)
                if front:
                    x_add_bias(m)
                    x_take_low(m)
                hidden_take_low(g, 2)
                hidden_take_low(g, 3)
                if front:
                    stage_w0(group_indices(VECTOR, 0, m))
                if middle:
                    experts_of = group_indices(VECTOR, 0, n)
                    l2_sum(n)
                    y2_take_low(n)
                low_take_rest(g, low2_high, low2_rested)
                low_take_low(g, low2_mid, low2_split)
                if front:
                    l0_sum(m)
                    rotate(m)
                if middle:
                    dve.wait_ge(stack2_full, g + 1)
                if front:
                    rotate_sum(m)
                elif middle:
                    dve.wait_ge(y2_split, n + 1)
                if middle:
                    stage_pick(experts_of)
                l3_sum(g)
                if front:
                    y1_take_rest(m)
                if middle:
                    low_take_rest(n, low1_high, low1_rested)
                    stage_ob(experts_of)
                    low_take_low(n, low1_mid, low1_split)
                if front:
                    y1_take_low(m)

            dve.wait_ge(pre_pe_done, 1)
            dve.wait_ge(exp_act, EXPERTS // 2)
            dve.wait_ge(exp_dve, EXPERTS // 2)
            experts_of = group_indices(VECTOR, 0, 0)
            stage_w0(experts_of)
            x_take_rest(0)
            x_add_bias(0)
            x_take_low(0)
            stage_pick(experts_of)
            stage_ob(experts_of)
            l0_sum(0)
            rotate(0)
            rotate_sum(0)
            y1_take_rest(0)
            y1_take_low(0)
            stage_w0(group_indices(VECTOR, 0, 1))
            x_take_rest(1)
            x_add_bias(1)
            x_take_low(1)
            l2_sum(0)
            y2_take_low(0)
            l0_sum(1)
            rotate(1)
            rotate_sum(1)
            y1_take_rest(1)
            y1_take_low(1)
            low_take_rest(0, low1_high, low1_rested)
            low_take_low(0, low1_mid, low1_split)
            with dve.Fori(0, GROUPS - 2) as g:
                body(g, True, True)
            body(GROUPS - 2, True, False)
            body(GROUPS - 1, False, False)

        @block.tensor
        def _(pe):
            pe.wait_ge(in_ident, 16)

            def free(j):
                if j >= 8:
                    pe.wait_ge(pre_high, HIGHS[j - 8])
                    pe.wait_ge(pre_rest, RESTS[j - 8])

            arrived = {
                "ia": (in_lora_a, 32), "ib": (in_lora_b, 16 * 2 * EXPERTS), "cib": (in_common, 64),
                "wi": (in_wi, 16), "wo": (in_wo, 16), "bias": (in_bias, 96),
            }
            for j, (how, name, n) in enumerate(JOBS):
                bank = banks[j % 8]
                free(j)
                if name in arrived and n == 0:
                    pe.wait_ge(*arrived[name])
                if name == "ia":
                    for h in range(HALVES):
                        last = nc.tensor.transpose(bank[:, P * h:P * (h + 1)], ia_nat[:, P * h:P * (h + 1)], ident[:])
                if name == "oa":
                    for i in range(4):
                        t = 4 * n + i
                        last = nc.tensor.transpose(bank[:, P * i:P * (i + 1)], oa_nat[:, P * t:P * (t + 1)], ident[:])
                if name == "ib":
                    for i in range(4):
                        last = nc.tensor.transpose(bank[:, P * i:P * (i + 1)], ib_nat[:, 4 * n + i, :], ident[:])
                if name == "ob":
                    for h in range(HALVES):
                        last = nc.tensor.transpose(bank[:, P * h:P * (h + 1)], ob_nat[:, h, :], ident[:])
                if name == "cib":
                    for i in range(4):
                        last = nc.tensor.transpose(bank[0:RANK, P * i:P * (i + 1)], cib_nat[:, 4 * n + i, :], ident[:])
                if name == "cob":
                    for h in range(HALVES):
                        last = nc.tensor.transpose(bank[0:RANK, P * h:P * (h + 1)], cob_nat[:, h, :], ident[:])
                if name == "bias":
                    pe.wait_ge(hot_done, 1)
                    for layer, (table, rows) in enumerate(((b0_nat, EXPERTS), (b2_nat, CATEGORIES))):
                        for h in range(HALVES):
                            c = BATCH * (HALVES * layer + h)
                            last = nc.tensor.matmul(bank[:, c:c + BATCH], table[0:rows, P * h:P * (h + 1)],
                                                    one_hot[0:rows, layer, :], start=True, stop=True)
                if name == "wi":
                    k, half = n // 2, n % 2
                    if n == 0:
                        pe.wait_ge(common_scaled, 1)
                        pe.wait_ge(pre_high, HIGHS[[i for i, job in enumerate(JOBS) if job[1] == "cob"][0]])
                    nc.tensor.matmul(bank[:, :], cia2[:, P * k:P * (k + 1)], cib_t[:, 512 * half:512 * half + 512],
                                     start=True, stop=True, skip_group_check=True)
                    for i in range(4):
                        last = nc.tensor.matmul(bank[:, P * i:P * (i + 1)], wi_nat[:, 4 * half + i, P * k:P * (k + 1)],
                                                ident[:], start=False, stop=True, skip_group_check=True)
                if name == "wo":
                    for i in range(2):
                        t = 2 * n + i
                        nc.tensor.matmul(bank[:, D * i:D * (i + 1)], coa2[:, P * t:P * (t + 1)], cob_t[:],
                                         start=True, stop=True, skip_group_check=True)
                        for h in range(HALVES):
                            last = nc.tensor.matmul(bank[:, D * i + P * h:D * i + P * (h + 1)],
                                                    wo_nat[:, h, P * t:P * (t + 1)], ident[:],
                                                    start=False, stop=True, skip_group_check=True)
                last.then_inc(pre_full, 1)

            pe.wait_ge(pre_high, len(JOBS))
            pe.wait_ge(pre_rest, RESTS[-1])
            pe.wait_ge(pre_low, 1)
            pe.wait_ge(pick_done, 1)
            with pe.Fori(0, EXPERTS // 2) as t:
                for i in range(2):
                    pe.wait_ge(in_w0[i], 16 * t + 16)
                for i in range(2):
                    for k in range(HALVES):
                        for h in range(HALVES):
                            last = nc.tensor.transpose(banks[i][:, D * k + P * h:D * k + P * (h + 1)],
                                                       w0_nat[:, i, h, P * k:P * (k + 1)], ident[:])
                last.then_inc(exp_w0_full, 1)
                for i in range(2):
                    select = put[:, bass.ds(2 * t + i, 1), :].rearrange("p o c -> p (o c)")
                    for half in range(2):
                        for part in range(PARTS):
                            nc.tensor.matmul(banks[2 + 2 * i + half][:, :], select[:, P * part:P * (part + 1)],
                                             ib_parts[:, part, 512 * half:512 * half + 512],
                                             start=(part == 0), stop=(part == PARTS - 1))
                for i in range(2):
                    select = put[:, bass.ds(2 * t + i, 1), :].rearrange("p o c -> p (o c)")
                    for part in range(PARTS):
                        last = nc.tensor.matmul(banks[6][:, D * i:D * (i + 1)], select[:, P * part:P * (part + 1)],
                                                ob_parts[:, part, :], start=(part == 0), stop=(part == PARTS - 1))
                last.then_inc(exp_full, 1)
                pe.wait_ge(exp_w0_rest, 2 * t + 2)
                pe.wait_ge(exp_act, t + 1)
                pe.wait_ge(exp_dve, t + 1)
                pe.nop()
            nc.tensor.transpose(banks[0][:, 0:P], ident[:], ident[:]).then_inc(pre_pe_done, 1)

            def turn_x(q):
                pe.wait_ge(x_in, 16 * q + 16)
                for t in range(TILES):
                    for h in range(HALVES):
                        last = nc.tensor.transpose(halves(turn_bank)[:, h, P * t:P * (t + 1)],
                                                   x_sb[:, t, P * h:P * (h + 1)], ident[:])
                last.then_inc(x_turned, 1)

            def per_sample(weights, parts, full):
                for h in range(HALVES):
                    for s in range(SPG):
                        count = 0
                        for w_part, a_part in PRODUCTS:
                            for k in range(HALVES):
                                c = D * k + P * h
                                last = nc.tensor.matmul(halves(front_bank)[:, h, SEQ * s:SEQ * (s + 1)],
                                                        weights[:, s, w_part, c:c + P],
                                                        parts[:, a_part, k, SEQ * s:SEQ * (s + 1)],
                                                        start=(count == 0), stop=(count == 2 * len(PRODUCTS) - 1))
                                count += 1
                last.then_inc(full, 1)

            def l0(q):
                pe.wait_ge(x_split, q + 1)
                pe.wait_ge(w0_staged, q + 1)
                per_sample(w0_stage, x_parts, l0_full)

            def l2(q):
                pe.wait_ge(y1_split, q + 1)
                for s in range(SPG):
                    pe.wait_ge(w2_split[s], q + 1)
                per_sample(w2_parts, y1_parts, l2_full)

            def three(bank, w_hi, w_lo, a_hi, a_lo, start=False, stop=False):
                nc.tensor.matmul(bank, w_lo, a_hi, start=start, stop=False, skip_group_check=True)
                nc.tensor.matmul(bank, w_hi, a_lo, start=False, stop=False, skip_group_check=True)
                return nc.tensor.matmul(bank, w_hi, a_hi, start=False, stop=stop, skip_group_check=True)

            def low1(q):
                pe.wait_ge(y2_split, q + 1)
                for k in range(HALVES):
                    last = three(low_bank, ia_hi[:, k, :], ia_lo[:, k, :], y2_hi[:, k, :], y2_lo[:, k, :],
                                 start=(k == 0), stop=(k == HALVES - 1))
                last.then_inc(low1_full, 1)

            def low2(g):
                for k in range(FT):
                    if k % 2 == 0:
                        pe.wait_ge(hid_split[k // 2], g + 1)
                    last = three(low_bank, oa_hi[:, k, :], oa_lo[:, k, :], hid_hi[:, k, :], hid_lo[:, k, :],
                                 start=(k == 0), stop=(k == FT - 1))
                last.then_inc(low2_full, 1)

            def pick_stack(q, split, full):
                pe.wait_ge(split, q + 1)
                for s in range(SPG):
                    for part in range(PARTS):
                        last = nc.tensor.matmul(stack_bank[:, SEQ * s:SEQ * (s + 1)],
                                                pick_stage[:, s, P * part:P * (part + 1)],
                                                low_parts[:, part, SEQ * s:SEQ * (s + 1)],
                                                start=(part == 0), stop=(part == PARTS - 1))
                last.then_inc(full, 1)

            def hidden_base(k):
                for i in range(2):
                    f = 2 * k + i
                    for h in range(HALVES):
                        three(halves(hidden_banks[k])[:, i, :], wi_hi[:, h, P * f:P * (f + 1)],
                              wi_lo[:, h, P * f:P * (f + 1)], y2_hi[:, h, :], y2_lo[:, h, :],
                              start=(i == 0 and h == 0), stop=(h == HALVES - 1))

            def hidden_lora(k):
                for i in range(2):
                    f = 2 * k + i
                    for s in range(SPG):
                        last = nc.tensor.matmul(halves(hidden_banks[k])[:, i, SEQ * s:SEQ * (s + 1)],
                                                ib_stage[:, s, P * f:P * (f + 1)], stack[:, SEQ * s:SEQ * (s + 1)],
                                                start=False, stop=True, skip_group_check=True)
                last.then_inc(hidden_full[k], 1)

            def out_half(h):
                for k in range(FT):
                    three(halves(out_bank)[:, h, :], wo_hi[:, k, P * h:P * (h + 1)], wo_lo[:, k, P * h:P * (h + 1)],
                          hid_hi[:, k, :], hid_lo[:, k, :], start=(h == 0 and k == 0), stop=(k == FT - 1))

            def out_lora(g):
                pe.wait_ge(stack2_done, g + 1)
                pe.wait_ge(ob_staged, g + 1)
                for h in range(HALVES):
                    for s in range(SPG):
                        last = nc.tensor.matmul(halves(out_bank)[:, h, SEQ * s:SEQ * (s + 1)],
                                                ob_stage[:, s, P * h:P * (h + 1)], stack[:, SEQ * s:SEQ * (s + 1)],
                                                start=False, stop=True, skip_group_check=True)
                last.then_inc(out_full, 1)

            def turn_out(g, q):
                pe.wait_ge(y3_done, g + 1)
                pe.wait_ge(x_biased, q + 1)
                for t in range(TILES):
                    for h in range(HALVES):
                        last = nc.tensor.transpose(turn_bank[:, D * t + P * h:D * t + P * (h + 1)],
                                                   y3[:, h, P * t:P * (t + 1)], ident[:])
                last.then_inc(out_turned, 1)

            def body(g, middle, front):
                n, m = g + 1, g + 2
                if front:
                    pe.wait_ge(out_taken, g + 1)
                    turn_x(m)
                hidden_base(2)
                pe.wait_ge(stack1_done, g + 1)
                pe.wait_ge(ib_staged, g + 1)
                hidden_lora(0)
                hidden_lora(1)
                hidden_base(3)
                hidden_lora(2)
                hidden_lora(3)
                if middle:
                    l2(n)
                low2(g)
                out_half(0)
                pick_stack(g, low2_split, stack2_full)
                if front:
                    pe.wait_ge(y2_done, n + 1)
                    l0(m)
                out_half(1)
                if middle:
                    pe.wait_ge(stack2_done, g + 1)
                    low1(n)
                out_lora(g)
                if middle:
                    hidden_base(0)
                turn_out(g, m if front else GROUPS - 1)
                if middle:
                    hidden_base(1)
                    pe.wait_ge(pick_staged, n + 1)
                    pick_stack(n, low1_split, stack1_full)

            turn_x(0)
            l0(0)
            pe.wait_ge(x_biased, 1)
            turn_x(1)
            l2(0)
            pe.wait_ge(y2_done, 1)
            l0(1)
            low1(0)
            hidden_base(0)
            hidden_base(1)
            pe.wait_ge(pick_staged, 1)
            pick_stack(0, low1_split, stack1_full)
            with pe.Fori(0, GROUPS - 2) as g:
                body(g, True, True)
            body(GROUPS - 2, True, False)
            body(GROUPS - 1, False, False)


_INS = ['x', 'itok_B_0_7', 'condB_deltat', 'itok_B_0_63', 'L0_cond_weight', 'L0_cond_bias',
        'L1_cond_amplitudes', 'L1_cond_frequencies', 'L2_cond_W', 'L2_cond_b', 'L3_cond_wi', 'L3_cond_wo',
        'L3_cond_common_wi_a', 'L3_cond_common_wi_b', 'L3_cond_common_wo_a', 'L3_cond_common_wo_b',
        'L3_cond_experts_wi_a', 'L3_cond_experts_wi_b', 'L3_cond_experts_wo_a', 'L3_cond_experts_wo_b']
_OUT = ((BATCH, SEQ, D), 'float32')


def kernel(**inputs):
    import concourse.bacc as _bacc
    from concourse.bass_utils import run_bass_kernel_spmd as _run

    nc = _bacc.Bacc("TRN2", target_bir_lowering=False, num_devices=1)
    arrays, args = {}, []
    given = {name: np.ascontiguousarray(inputs[name]) for name in _INS}
    given["identity"] = np.eye(P, dtype=np.float32)
    given["place"] = stack_constants()
    given["small"] = small_constants()
    for name, a in given.items():
        arrays[f"in_{name}_dram"] = a
        args.append(nc.dram_tensor(f"in_{name}_dram", a.shape, mybir.dt.from_np(a.dtype), kind="ExternalInput").ap())
    args.append(nc.dram_tensor("out_0_dram", _OUT[0], FP32, kind="ExternalOutput").ap())
    cond_resid_kernel(nc, *args)
    r = _run(nc, [arrays], core_ids=[0])
    return r.results[0]["out_0_dram"]
```

```python
from contextlib import ExitStack

import numpy as np

import concourse.bass as bass
from concourse import mybir

FP32 = mybir.dt.float32
F32R = mybir.dt.float32r
BF16 = mybir.dt.bfloat16
I32 = mybir.dt.int32
ALU = mybir.AluOpType
ACT = mybir.ActivationFunctionType

P = 128
BATCH, SEQ, D = 128, 64, 256
F = 1024
EXPERTS, RANK = 8, 16
CATEGORIES = 64
SPG = 4
GT = SPG * SEQ
GROUPS = BATCH // SPG
TILES = GT // P
HALVES = D // P
FT = F // P
PAIRS = FT // 2
PARTS = 3
PRODUCTS = [(2, 0), (0, 2), (1, 1), (1, 0), (0, 1), (0, 0)]
STACK_ROW = {(0, 2): 0, (1, 1): 16, (0, 1): 32, (2, 0): 48, (1, 0): 64, (0, 0): 80}
STACK_LOWS, STACK_MIDS, STACK_ROWS = 16, 48, 96
ALPHA = 2.0
REST_PLACES = 3


def spread_constants():
    spread = np.zeros((4 * RANK, STACK_ROWS), np.float32)
    for row in STACK_ROW.values():
        for r in range(RANK):
            spread[r::RANK, row + r] = 1.0
    return spread


def number_constants():
    return np.arange(P, dtype=np.float32).reshape(P, 1)


def cond_resid_kernel(nc, x, experts, delta_t, cats, w0, b0, amplitudes, frequencies, w2, b2, wi, wo,
                      common_wi_a, common_wi_b, common_wo_a, common_wo_b,
                      experts_wi_a, experts_wi_b, experts_wo_a, experts_wo_b,
                      identity, spread, numbers, out):
    x_rows = x.rearrange("b s d -> (b s) d").rearrange("(q t p) d -> q p t d", t=TILES, p=P)
    out_rows = out.rearrange("b s d -> (b s) d").rearrange("(q t p) d -> q p t d", t=TILES, p=P)
    parts_dram = nc.dram_tensor("parts_scratch", (PARTS, EXPERTS * RANK, F + D), BF16, kind="Internal").ap()
    rotation_dram = nc.dram_tensor("rotation_scratch", (2, BATCH * SEQ), FP32, kind="Internal").ap()

    ctx = ExitStack()
    with ctx:
        def sb(name, shape, dtype=FP32, stack=ctx):
            return stack.enter_context(nc.sbuf_tensor(name, shape, dtype))

        def sem(name):
            return ctx.enter_context(nc.semaphore(name))

        ident = sb("ident", [P, P])
        numbers_sb = sb("numbers_sb", [P, 1])
        wi_hi, wi_lo = (sb(f"wi_{n}", [P, HALVES, F], F32R) for n in ("hi", "lo"))
        wo_hi, wo_lo = (sb(f"wo_{n}", [P, FT, D], F32R) for n in ("hi", "lo"))
        factors = sb("factors", [P, EXPERTS, FT + HALVES, 2 * RANK], F32R)
        w0_parts = sb("w0_parts", [P, EXPERTS, PARTS, HALVES * D], BF16)
        lora_stack = sb("lora_stack", [P, EXPERTS, F + D], BF16)
        spread_sb = sb("spread_sb", [4 * RANK, STACK_ROWS], F32R)
        bias = sb("bias", [P, 2 * HALVES, BATCH])
        index_given = sb("index_given", [1, 2, BATCH], I32)
        index = sb("index", [1, 2, BATCH], I32)

        x_sb = sb("x_sb", [P, TILES, D])
        x_rest = sb("x_rest", [P, HALVES, GT])
        y2 = sb("y2", [P, 2, HALVES, GT])
        y1_bias = sb("y1_bias", [P, HALVES, GT])
        rotation = sb("rotation", [P, 2, GT])
        w2_raw = sb("w2_raw", [P, SPG, HALVES * D])
        factors_stage = sb("factors_stage", [P, SPG, FT + HALVES, 2 * RANK], F32R)
        y2_pair = sb("y2_pair", [P, HALVES, 2, GT], F32R)

        scratch = ExitStack()
        wi_nat = sb("wi_nat", [P, FT, D], FP32, scratch)
        w0_nat = sb("w0_nat", [P, EXPERTS, HALVES, D], FP32, scratch)
        ib_nat = sb("ib_nat", [P, FT, P], FP32, scratch)
        ob_nat = sb("ob_nat", [P, HALVES, P], FP32, scratch)
        cia = sb("cia", [RANK, D], FP32, scratch)
        cib_nat = sb("cib_nat", [P, FT, RANK], FP32, scratch)
        cob_nat = sb("cob_nat", [P, HALVES, RANK], FP32, scratch)
        cia2 = sb("cia2", [RANK, D], FP32, scratch)
        cib_t = sb("cib_t", [RANK, F], FP32, scratch)
        b0_nat = sb("b0_nat", [EXPERTS, D], FP32, scratch)
        b2_nat = sb("b2_nat", [CATEGORIES, D], FP32, scratch)
        index_all = sb("index_all", [CATEGORIES, 2, BATCH], I32, scratch)
        index_f = sb("index_f", [CATEGORIES, 2, BATCH], FP32, scratch)
        one_hot = sb("one_hot", [CATEGORIES, 2, BATCH], FP32, scratch)
        wo_nat = sb("wo_nat", [P, HALVES, F], FP32, scratch)
        ia_nat = sb("ia_nat", [P, D], FP32, scratch)
        oa_nat = sb("oa_nat", [P, F], FP32, scratch)
        coa2 = sb("coa2", [RANK, F], FP32, scratch)
        cob_t = sb("cob_t", [RANK, D], FP32, scratch)
        coa = sb("coa", [RANK, F], FP32, scratch)
        rest = sb("rest", [P, REST_PLACES, 512], FP32, scratch)
        rot = sb("rot", [P, 14, SEQ], FP32, scratch)
        dt_sb = sb("dt_sb", [P, 1], FP32, scratch)
        spread_in = sb("spread_in", [4 * RANK, STACK_ROWS], FP32, scratch)
        lora_parts = sb("lora_parts", [P, PARTS, F + D], BF16, scratch)
        scratch.close()

        w0_stage = sb("w0_stage", [P, SPG, PARTS, HALVES * D], BF16)
        w2_parts = sb("w2_parts", [P, SPG, PARTS, HALVES * D], BF16)
        x_parts = sb("x_parts", [P, PARTS, HALVES, GT], BF16)
        x_bias = sb("x_bias", [P, HALVES, GT])
        y0 = sb("y0", [P, HALVES, GT])
        y0_cos = sb("y0_cos", [P, HALVES, GT])
        y0_sin = sb("y0_sin", [P, HALVES, GT])
        y1 = sb("y1", [P, HALVES, GT])
        y1_rest = sb("y1_rest", [P, HALVES, GT])
        y1_parts = sb("y1_parts", [P, PARTS, HALVES, GT], BF16)
        low = sb("low", [2 * RANK, GT])
        low_pair = sb("low_pair", [4 * RANK, GT], F32R)
        stack_rest = sb("stack_rest", [P, GT])
        stack = sb("stack", [P, GT], BF16)
        y3 = sb("y3", [P, HALVES, GT])
        ib_stage = sb("ib_stage", [P, SPG, F], BF16)
        ob_stage = sb("ob_stage", [P, SPG, D], BF16)
        hid_pair = sb("hid_pair", [P, FT, 2, GT], F32R)
        out_sb = sb("out_sb", [P, TILES, D])

        banks = [ctx.enter_context(nc.psum_tensor(f"bank{n}", [P, 512], FP32)) for n in range(8)]

        def halves(bank):
            return bank[:, :].rearrange("p (h t) -> p h t", h=HALVES)

        turn_bank = banks[0]
        front_bank = banks[1]
        hidden_banks = banks[2:6]
        out_bank = banks[6]
        low_bank = banks[7]
        stack_bank = low_bank[0:STACK_ROWS, 0:GT]

        in_ident = sem("in_ident")
        in_index = sem("in_index")
        index_ready = sem("index_ready")
        in_rot = sem("in_rot")
        in_ia = sem("in_ia")
        in_oa = sem("in_oa")
        in_lora_b = sem("in_lora_b")
        in_common = sem("in_common")
        in_wi = [sem("in_wi0"), sem("in_wi1")]
        in_wo = sem("in_wo")
        in_bias = sem("in_bias")
        in_numbers = sem("in_numbers")
        in_spread = sem("in_spread")
        in_w0 = [sem(f"in_w0_{i}") for i in range(EXPERTS)]
        rot_step = sem("rot_step")
        rot_sines = sem("rot_sines")
        rot_angles = sem("rot_angles")
        rot_trig = sem("rot_trig")
        rot_saved = sem("rot_saved")
        spread_ready = sem("spread_ready")
        parts_saved = sem("parts_saved")
        in_stack = sem("in_stack")
        hot_cast = sem("hot_cast")
        hot_done = sem("hot_done")
        cia_scaled = sem("cia_scaled")
        coa_scaled = sem("coa_scaled")
        pre_full = sem("pre_full")
        pre_high = sem("pre_high")
        pre_rest = sem("pre_rest")
        pre_mid = sem("pre_mid")
        pre_low = sem("pre_low")

        x_in = sem("x_in")
        rotation_in = sem("rotation_in")
        w2_in = [sem(f"w2_in{s}") for s in range(SPG)]
        out_stored = sem("out_stored")
        x_turned = sem("x_turned")
        l0_full = sem("l0_full")
        l2_full = sem("l2_full")
        low1_full = sem("low1_full")
        low2_full = sem("low2_full")
        spread1_full = sem("spread1_full")
        spread2_full = sem("spread2_full")
        hidden_full = [sem(f"hidden_full{k}") for k in range(PAIRS)]
        out_full = sem("out_full")
        out_turned = sem("out_turned")
        x_high = sem("x_high")
        x_rested = sem("x_rested")
        x_biased = sem("x_biased")
        x_mid = sem("x_mid")
        x_split = sem("x_split")
        y0_done = sem("y0_done")
        y0_cos_done = sem("y0_cos_done")
        y0_sin_done = sem("y0_sin_done")
        y1_done = sem("y1_done")
        y1_high = sem("y1_high")
        y1_rested = sem("y1_rested")
        y1_mid = sem("y1_mid")
        y1_split = sem("y1_split")
        y1_biased = sem("y1_biased")
        y2_done = sem("y2_done")
        y2_high = sem("y2_high")
        y2_split = sem("y2_split")
        low1_summed, low1_high, low1_split = (sem(f"low1_{n}") for n in ("summed", "high", "split"))
        low2_summed, low2_high, low2_split = (sem(f"low2_{n}") for n in ("summed", "high", "split"))
        stack1_high, stack1_rested, stack1_mid, stack1_done = (
            sem(f"stack1_{n}") for n in ("high", "rested", "mid", "done"))
        stack2_high, stack2_rested, stack2_mid, stack2_done = (
            sem(f"stack2_{n}") for n in ("high", "rested", "mid", "done"))
        hid_high = [sem(f"hid_high{k}") for k in range(PAIRS)]
        hid_split = [sem(f"hid_split{k}") for k in range(PAIRS)]
        y3_done = sem("y3_done")
        out_taken = sem("out_taken")
        w2_high = [sem(f"w2_high{s}") for s in range(SPG)]
        w2_rested = [sem(f"w2_rested{s}") for s in range(SPG)]
        w2_mid = [sem(f"w2_mid{s}") for s in range(SPG)]
        w2_split = [sem(f"w2_split{s}") for s in range(SPG)]
        w0_staged = sem("w0_staged")
        ib_staged = sem("ib_staged")
        ob_staged = sem("ob_staged")
        factors_staged = sem("factors_staged")

        SPLIT2, SPLIT3, COPY = "two float32r parts", "three bfloat16 parts", "a copy"
        JOBS = []
        W0, WI, WO = ([(how, name, n) for n in range(count)] for how, name, count in
                      ((SPLIT3, "w0", EXPERTS), (SPLIT2, "wi", 4), (SPLIT2, "wo", FT // 2)))
        JOBS += [W0[0], (COPY, "cib", 0), W0[1], (COPY, "cib", 1), (COPY, "cob", 0)]
        JOBS += [WI[0], W0[2], WI[1], W0[3], WI[2], W0[4], WI[3], W0[5], (COPY, "bias", 0), W0[6], W0[7]]
        JOBS += [(SPLIT3, "ib", 0), (SPLIT3, "ib", 1), (SPLIT3, "ob", 0)]
        EARLY = len(JOBS)
        JOBS += [WO[0], WO[1], WO[2], WO[3], (SPLIT2, "oa", 0), (SPLIT2, "oa", 1), (SPLIT2, "ia", 0)]
        JOB_BANK = [j % 8 if j < 16 else 2 + (j - 16) % 6 for j in range(len(JOBS))]

        def job(name, n=0):
            return [i for i, (_, *which) in enumerate(JOBS) if which == [name, n]][0]

        THREES = [j for j in range(len(JOBS)) if JOBS[j][0] == SPLIT3]
        RESTS = [sum(JOBS[i][0] != COPY for i in range(j + 1)) for j in range(len(JOBS))]
        MID_LAG, LOW_LAG = 1, 2

        def job_views(j):
            how, name, n = JOBS[j]
            bank = banks[JOB_BANK[j]]
            if name == "w0":
                return bank[:, :], [w0_parts[:, n, q, :] for q in range(PARTS)]
            if name == "ia":
                return (bank[:, 0:256].rearrange("p (h e r) -> p h e r", h=HALVES, e=EXPERTS),
                        [factors[:, :, FT:FT + HALVES, RANK * q:RANK * (q + 1)].rearrange("p e h r -> p h e r")
                         for q in range(2)])
            if name == "oa":
                return (bank[:, :].rearrange("p (k e r) -> p k e r", k=4, e=EXPERTS),
                        [factors[:, :, 4 * n:4 * n + 4, RANK * q:RANK * (q + 1)].rearrange("p e k r -> p k e r")
                         for q in range(2)])
            if name == "ib":
                return bank[:, :], [lora_parts[:, q, 512 * n:512 * (n + 1)] for q in range(PARTS)]
            if name == "ob":
                return bank[:, 0:D], [lora_parts[:, q, F:F + D] for q in range(PARTS)]
            if name == "cib":
                return bank[0:RANK, :], (cib_t[:, 512 * n:512 * (n + 1)],)
            if name == "cob":
                return bank[0:RANK, 0:D], (cob_t[:, :],)
            if name == "bias":
                return bank[:, :].rearrange("p (h b) -> p h b", h=2 * HALVES), (bias[:],)
            if name == "wi":
                k, c = n % 2, slice(512 * (n // 2), 512 * (n // 2) + 512)
                return bank[:, :], (wi_hi[:, k, c], wi_lo[:, k, c])
            if name == "wo":
                t = slice(2 * n, 2 * n + 2)
                return bank[:, :].rearrange("p (k d) -> p k d", k=2), (wo_hi[:, t, :], wo_lo[:, t, :])

        SP, SCALAR, VECTOR = mybir.EngineType.SP, mybir.EngineType.Activation, mybir.EngineType.DVE

        def job_rest(j):
            columns = D if JOBS[j][1] == "ob" else 512
            return rest[:, THREES.index(j) % REST_PLACES, 0:columns]

        def group_indices(engine, which, q):
            _, values = nc.values_load_multi_w_load_instructions(
                index[0:1, which, bass.ds(SPG * q, SPG)], engines=(engine,), min_val=0,
                max_val=(EXPERTS, CATEGORIES)[which] - 1,
                skip_runtime_bounds_check_because="VectorE clamped the indices to this range")
            return values

        block = ctx.enter_context(nc.Block())

        @block.sync
        def _(sp):
            def load_w0(e):
                sp.dma_start(w0_nat[:, e], w0[e].rearrange("(h p) d -> p h d", p=P)).then_inc(in_w0[e], 16)

            def load_lora_b(nat, given, t):
                sp.dma_start(nat[:, t, :].rearrange("p (e r) -> p e r", e=EXPERTS),
                             given[:, P * t:P * (t + 1), :].rearrange("e p r -> p e r")).then_inc(in_lora_b, 16)

            def load_wi(half):
                t = slice(4 * half, 4 * half + 4)
                sp.dma_start(wi_nat[:, t], wi.rearrange("(t p) d -> p t d", p=P)[:, t]).then_inc(in_wi[half], 16)

            sp.dma_start(ident[:], identity).then_inc(in_ident, 16)
            load_w0(0)
            load_wi(0)
            sp.dma_start(dt_sb[:], delta_t.rearrange("(b o) -> b o", o=1)).then_inc(in_rot, 16)
            sp.dma_start(rot[:, 0, :], amplitudes.partition_broadcast(P)).then_inc(in_rot, 16)
            load_w0(1)
            sp.dma_start(rot[:, 1, :], frequencies.partition_broadcast(P)).then_inc(in_rot, 16)
            load_w0(2)
            load_w0(3)
            load_wi(1)
            sp.dma_start(index_given[:, 0, :], experts.rearrange("(o b) -> o b", o=1)).then_inc(in_index, 16)
            sp.dma_start(index_given[:, 1, :], cats.rearrange("(o b) -> o b", o=1)).then_inc(in_index, 16)
            load_w0(4)
            load_w0(5)
            sp.dma_start(numbers_sb[:], numbers).then_inc(in_numbers, 16)
            sp.dma_start(spread_in[:], spread).then_inc(in_spread, 16)
            sp.dma_start(index_all[:, 0, :], experts.partition_broadcast(CATEGORIES)).then_inc(in_bias, 16)
            sp.dma_start(index_all[:, 1, :], cats.partition_broadcast(CATEGORIES)).then_inc(in_bias, 16)
            sp.dma_start(b0_nat[:], b0).then_inc(in_bias, 16)
            sp.dma_start(b2_nat[:], b2).then_inc(in_bias, 16)
            load_w0(6)
            load_w0(7)
            for t in range(FT):
                load_lora_b(ib_nat, experts_wi_b, t)
            for t in range(HALVES):
                load_lora_b(ob_nat, experts_wo_b, t)
            sp.dma_start(x_sb[:], x_rows[0]).then_inc(x_in, 16)
            sp.dma_start(wo_nat[:], wo.rearrange("(t p) f -> p t f", p=P)).then_inc(in_wo, 16)
            sp.dma_start(ia_nat[:], experts_wi_a.rearrange("e r d -> (e r) d")).then_inc(in_ia, 16)
            sp.dma_start(oa_nat[:], experts_wo_a.rearrange("e r f -> (e r) f")).then_inc(in_oa, 16)

            def load_w2(q, s, category):
                sp.dma_start(w2_raw[:, s, :].rearrange("p (h d) -> p h d", h=HALVES),
                             w2[bass.ds(category, 1)].rearrange("o (h p) d -> p (o h) d", p=P)
                             ).then_inc(w2_in[s], 16)

            def load_rotation(q):
                sp.dma_start(rotation[:], rotation_dram[:, bass.ds(GT * q, GT)].partition_broadcast(P)
                             ).then_inc(rotation_in, 16)

            def load_x(q):
                sp.wait_ge(x_turned, q)
                sp.dma_start(x_sb[:], x_rows[bass.ds(q, 1)].rearrange("o p t d -> p (o t) d")).then_inc(x_in, 16)

            sp.wait_ge(index_ready, 1)
            categories = group_indices(SP, 1, 0)
            for s in range(SPG):
                load_w2(0, s, categories[s])
            load_x(1)
            sp.wait_ge(rot_trig, 1)
            sp.dma_start(rotation_dram[0].rearrange("(b s) -> b s", s=SEQ), rot[:, 12, :]).then_inc(rot_saved, 16)
            sp.dma_start(rotation_dram[1].rearrange("(b s) -> b s", s=SEQ), rot[:, 13, :]).then_inc(rot_saved, 16)
            sp.wait_ge(rot_saved, 32)
            load_rotation(0)
            sp.wait_ge(pre_high, job("ob") + 1)
            sp.wait_ge(pre_mid, len(THREES))
            sp.wait_ge(pre_low, len(THREES))
            sp.dma_start(parts_dram.rearrange("q p c -> p q c"), lora_parts[:]).then_inc(parts_saved, 16)
            sp.wait_ge(parts_saved, 16)
            for (w_part, _), row in STACK_ROW.items():
                sp.dma_start(lora_stack[row:row + RANK],
                             parts_dram[w_part].rearrange("(e r) c -> r e c", r=RANK)).then_inc(in_stack, 16)

            def load_categories(q):
                categories = group_indices(SP, 1, q)
                for s in range(SPG):
                    sp.wait_ge(w2_split[s], q)
                    load_w2(q, s, categories[s])

            def load_factors(q):
                sp.wait_ge(y0_sin_done, q)
                load_rotation(q)

            def store(g):
                sp.wait_ge(out_taken, g + 2)
                sp.dma_start(out_rows[bass.ds(g, 1)].rearrange("o p t d -> p (o t) d"), out_sb[:]
                             ).then_inc(out_stored, 16)

            load_factors(1)
            load_categories(1)
            load_x(2)
            load_factors(2)
            with sp.Fori(0, GROUPS - 3) as g:
                load_x(g + 3)
                load_categories(g + 2)
                load_factors(g + 3)
                store(g)
            load_categories(GROUPS - 1)
            for g in range(GROUPS - 3, GROUPS):
                store(g)
            sp.wait_ge(out_stored, 16 * (GROUPS + 1))

        @block.gpsimd
        def _(pool):
            steps = [0]

            def then(instruction):
                steps[0] += 1
                instruction.then_inc(rot_step, 1)
                pool.wait_ge(rot_step, steps[0])

            TWO_PI = 2.0 * np.pi
            ROUND = 1.5 * 2.0 ** 23
            C1 = 6.28125
            C2 = float(np.float32(np.round((TWO_PI - C1) * 2.0 ** 21) / 2.0 ** 21))
            C3 = float(np.float32(TWO_PI - C1 - C2))
            LIMIT = 3.1415925
            pool.wait_ge(in_rot, 48)
            nc.gpsimd.tensor_tensor(rot[:, 2, :], rot[:, 0, :], dt_sb[:, 0:1].to_broadcast([P, SEQ]), ALU.pow)
            then(nc.gpsimd.tensor_tensor(rot[:, 3, :], rot[:, 1, :], dt_sb[:, 0:1].to_broadcast([P, SEQ]), ALU.mult))
            for at, offset, shift in ((4, 0.0, 0.0), (5, 0.25, 0.5 * np.pi)):
                angle = 8 if at == 4 else 9
                then(nc.gpsimd.tensor_scalar(rot[:, at, :], rot[:, 3, :], float(1.0 / TWO_PI), offset, ALU.mult, ALU.add))
                then(nc.gpsimd.tensor_scalar(rot[:, 6, :], rot[:, at, :], ROUND, None, ALU.add))
                then(nc.gpsimd.tensor_scalar(rot[:, 7, :], rot[:, 6, :], -ROUND, None, ALU.add))
                before = rot[:, 3, :]
                for piece, to in ((C1, at), (C2, at), (C3, at)):
                    then(nc.gpsimd.tensor_scalar(rot[:, 6, :], rot[:, 7, :], -piece, None, ALU.mult))
                    then(nc.gpsimd.tensor_tensor(rot[:, to, :], rot[:, 6, :], before, ALU.add))
                    before = rot[:, to, :]
                then(nc.gpsimd.tensor_scalar(rot[:, 6, :], rot[:, at, :], shift, LIMIT, ALU.add, ALU.min))
                last = nc.gpsimd.tensor_scalar(rot[:, angle, :], rot[:, 6, :], -LIMIT, None, ALU.max)
                if at == 4:
                    then(last)
            last.then_inc(rot_angles, 1)
            pool.wait_ge(in_common, 64)
            nc.gpsimd.tensor_scalar(coa2[:], coa[:], ALPHA, 1.0, ALU.mult, ALU.mult).then_inc(coa_scaled, 1)
            pool.wait_ge(in_spread, 16)
            nc.gpsimd.tensor_scalar(spread_sb[:], spread_in[:], ALPHA, 1.0, ALU.mult, ALU.mult).then_inc(spread_ready, 1)
            pool.wait_ge(rot_sines, 1)
            then(nc.gpsimd.tensor_tensor(rot[:, 4, :], rot[:, 2, :], rot[:, 11, :], ALU.mult))
            nc.gpsimd.tensor_scalar(rot[:, 12, :], rot[:, 4, :], 1.0, None, ALU.add)
            nc.gpsimd.tensor_tensor(rot[:, 13, :], rot[:, 2, :], rot[:, 10, :], ALU.mult).then_inc(rot_trig, 1)

            def w2_take_high(q):
                for s in range(SPG):
                    pool.wait_ge(w2_high[s], q + 1)
                    nc.gpsimd.tensor_tensor(w2_raw[:, s, :], w2_raw[:, s, :], w2_parts[:, s, 0, :],
                                            ALU.subtract).then_inc(w2_rested[s], 1)

            def w2_take_mid(q):
                for s in range(SPG):
                    pool.wait_ge(w2_mid[s], q + 1)
                    nc.gpsimd.tensor_tensor(w2_parts[:, s, 2, :], w2_raw[:, s, :], w2_parts[:, s, 1, :],
                                            ALU.subtract).then_inc(w2_split[s], 1)

            def add_bias2(q):
                pool.wait_ge(y1_done, q + 1)
                b = bias[:, HALVES:2 * HALVES, bass.ds(SPG * q, SPG)].unsqueeze(3)
                nc.gpsimd.tensor_tensor(y1_bias[:].rearrange("p h (s t) -> p h s t", s=SPG),
                                        y1[:].rearrange("p h (s t) -> p h s t", s=SPG),
                                        b.to_broadcast([P, HALVES, SPG, SEQ]), ALU.add).then_inc(y1_biased, 1)

            w2_take_high(0)
            w2_take_mid(0)
            add_bias2(0)
            w2_take_high(1)
            w2_take_mid(1)
            add_bias2(1)
            with pool.Fori(0, GROUPS - 2) as g:
                w2_take_high(g + 2)
                w2_take_mid(g + 2)
                add_bias2(g + 2)

        @block.scalar
        def _(act):
            act.dma_start(cib_nat[:], common_wi_b.rearrange("(t p) r -> p t r", p=P)).then_inc(in_common, 16)
            act.dma_start(cob_nat[:], common_wo_b.rearrange("(t p) r -> p t r", p=P)).then_inc(in_common, 16)
            act.dma_start(cia[:], common_wi_a).then_inc(in_common, 16)
            act.dma_start(coa[:], common_wo_a).then_inc(in_common, 16)

            def take_jobs(first, last):
                for j in range(first, last):
                    how, name, n = JOBS[j]
                    if (name, n) == ("wi", 0):
                        act.wait_ge(in_common, 64)
                        nc.scalar.mul(cia2[:], cia[:], ALPHA).then_inc(cia_scaled, 1)
                    bank, parts = job_views(j)
                    act.wait_ge(pre_full, j + 1)
                    nc.scalar.copy(parts[0], bank).then_inc(pre_high, 1)
                    if (name, n) == ("w0", 6):
                        act.wait_ge(rot_angles, 1)
                        nc.scalar.activation(rot[:, 10, :], rot[:, 8, :], ACT.Sin)
                        nc.scalar.activation(rot[:, 11, :], rot[:, 9, :], ACT.Sin).then_inc(rot_sines, 1)
                    for i in THREES:
                        if i + MID_LAG == j < EARLY or j == EARLY - 1 < i + MID_LAG:
                            act.wait_ge(pre_rest, RESTS[i])
                            nc.scalar.copy(job_views(i)[1][1], job_rest(i)).then_inc(pre_mid, 1)

            take_jobs(0, EARLY)

            def x_take_high(q):
                act.wait_ge(x_turned, q + 1)
                nc.scalar.copy(x_parts[:, 0], halves(turn_bank)).then_inc(x_high, 1)

            def x_take_mid(q):
                act.wait_ge(x_rested, q + 1)
                nc.scalar.copy(x_parts[:, 1], x_rest[:]).then_inc(x_mid, 1)

            def y1_take_high(q):
                act.wait_ge(y1_done, q + 1)
                nc.scalar.copy(y1_parts[:, 0], y1[:]).then_inc(y1_high, 1)

            def y1_take_mid(q):
                act.wait_ge(y1_rested, q + 1)
                nc.scalar.copy(y1_parts[:, 1], y1_rest[:]).then_inc(y1_mid, 1)

            def y2_take_high(q):
                act.wait_ge(y2_done, q + 1)
                nc.scalar.copy(y2_pair[:, :, 0], y2[:, bass.ds(q % 2, 1)].rearrange("p o h t -> p (o h) t")
                               ).then_inc(y2_high, 1)

            def low_take_high(q, summed, high):
                act.wait_ge(summed, q + 1)
                nc.scalar.copy(low_pair[0:2 * RANK], low[:]).then_inc(high, 1)

            def stack_take_high(q, full, high):
                act.wait_ge(full, q + 1)
                nc.scalar.copy(stack[0:STACK_ROWS], stack_bank).then_inc(high, 1)

            def stack_take_mid(q, rested, mid):
                act.wait_ge(rested, q + 1)
                nc.scalar.copy(stack[0:STACK_MIDS], stack_rest[0:STACK_MIDS]).then_inc(mid, 1)

            def hidden_take_high(g, k):
                act.wait_ge(hidden_full[k], g + 1)
                nc.scalar.activation(hid_pair[:, 2 * k:2 * k + 2, 0, :], halves(hidden_banks[k]), ACT.Relu
                                     ).then_inc(hid_high[k], 1)

            def w2_take_high(q, samples=range(SPG)):
                for s in samples:
                    act.wait_ge(w2_in[s], 16 * q + 16)
                    nc.scalar.copy(w2_parts[:, s, 0, :], w2_raw[:, s, :]).then_inc(w2_high[s], 1)

            def w2_take_mid(q, samples=range(SPG)):
                for s in samples:
                    act.wait_ge(w2_rested[s], q + 1)
                    nc.scalar.copy(w2_parts[:, s, 1, :], w2_raw[:, s, :]).then_inc(w2_mid[s], 1)

            def take_out(g):
                act.wait_ge(out_turned, g + 1)
                act.wait_ge(out_stored, 16 * g + 16)
                nc.scalar.copy(out_sb[:], turn_bank[:, :].rearrange("p (t d) -> p t d", t=TILES)
                               ).then_inc(out_taken, 1)

            def stage_ib(experts_of, samples):
                for s in samples:
                    last = nc.scalar.copy(ib_stage[0:STACK_ROWS, s, :],
                                          lora_stack[0:STACK_ROWS, bass.ds(experts_of[s], 1), 0:F].rearrange("p o c -> p (o c)"))
                last.then_inc(ib_staged, len(samples))

            def body(g, middle, front):
                n, m = g + 1, g + 2
                if front:
                    x_take_high(m)
                hidden_take_high(g, 0)
                hidden_take_high(g, 1)
                if front:
                    x_take_mid(m)
                hidden_take_high(g, 2)
                hidden_take_high(g, 3)
                if middle:
                    experts_of = group_indices(SCALAR, 0, n)
                    stage_ib(experts_of, [0, 1])
                    y2_take_high(n)
                if front:
                    w2_take_high(n + 1, [0, 1])
                low_take_high(g, low2_summed, low2_high)
                if front:
                    w2_take_high(n + 1, [2, 3])
                stack_take_high(g, spread2_full, stack2_high)
                stack_take_mid(g, stack2_rested, stack2_mid)
                if front:
                    w2_take_mid(n + 1)
                if middle:
                    stage_ib(experts_of, [2, 3])
                if front:
                    y1_take_high(m)
                if middle:
                    low_take_high(n, low1_summed, low1_high)
                    stack_take_high(n, spread1_full, stack1_high)
                take_out(g)
                if middle:
                    stack_take_mid(n, stack1_rested, stack1_mid)
                if front:
                    y1_take_mid(m)

            act.wait_ge(pre_full, EARLY)
            act.wait_ge(index_ready, 1)
            act.sem_inc(out_taken, 1)
            act.sem_inc(out_stored, 16)
            x_take_high(0)
            w2_take_high(0, [0])
            x_take_mid(0)
            w2_take_high(0, [1, 2, 3])
            take_jobs(EARLY, EARLY + 4)
            w2_take_mid(0)
            x_take_high(1)
            y1_take_high(0)
            x_take_mid(1)
            y1_take_mid(0)
            take_jobs(EARLY + 4, len(JOBS))
            y2_take_high(0)
            w2_take_high(1)
            act.wait_ge(pre_full, len(JOBS))
            act.wait_ge(rot_saved, 32)
            act.wait_ge(parts_saved, 16)
            act.wait_ge(spread_ready, 1)
            act.wait_ge(in_stack, 16 * len(STACK_ROW))
            low_take_high(0, low1_summed, low1_high)
            w2_take_mid(1, [0, 1])
            stack_take_high(0, spread1_full, stack1_high)
            stack_take_mid(0, stack1_rested, stack1_mid)
            y1_take_high(1)
            w2_take_mid(1, [2, 3])
            y1_take_mid(1)
            with act.Fori(0, GROUPS - 2) as g:
                body(g, True, True)
            body(GROUPS - 2, True, False)
            body(GROUPS - 1, False, False)

        @block.vector
        def _(dve):
            def index_rows():
                dve.wait_ge(in_index, 32)
                nc.vector.tensor_scalar(index[:, 0, :], index_given[:, 0, :], 0, EXPERTS - 1, ALU.max, ALU.min)
                nc.vector.tensor_scalar(index[:, 1, :], index_given[:, 1, :], 0, CATEGORIES - 1, ALU.max, ALU.min
                                        ).then_inc(index_ready, 1)
                dve.wait_ge(in_bias, 64)
                dve.wait_ge(in_numbers, 16)
                nc.vector.tensor_copy(index_f[:], index_all[:]).then_inc(hot_cast, 1)
                dve.wait_ge(hot_cast, 1)
                nc.vector.tensor_scalar(one_hot[:], index_f[:], numbers_sb[0:CATEGORIES, 0:1], None, ALU.is_equal
                                        ).then_inc(hot_done, 1)

            def take_jobs(first, last):
                for j in range(first, last):
                    how, name, n = JOBS[j]
                    if (name, n) == ("wi", 3):
                        index_rows()
                    if how != COPY:
                        bank, parts = job_views(j)
                        dve.wait_ge(pre_high, j + 1)
                    if how == SPLIT2:
                        nc.vector.tensor_tensor(parts[1], bank, parts[0], ALU.subtract).then_inc(pre_rest, 1)
                    if how == SPLIT3:
                        order = THREES.index(j)
                        if order >= REST_PLACES:
                            dve.wait_ge(pre_low, order - REST_PLACES + 1)
                        nc.vector.tensor_tensor(job_rest(j), bank, parts[0], ALU.subtract).then_inc(pre_rest, 1)
                    for i in THREES:
                        if i + LOW_LAG == j < EARLY or j == EARLY - 1 < i + LOW_LAG:
                            dve.wait_ge(pre_mid, THREES.index(i) + 1)
                            parts = job_views(i)[1]
                            nc.vector.tensor_tensor(parts[2], job_rest(i), parts[1], ALU.subtract).then_inc(pre_low, 1)

            take_jobs(0, EARLY)

            def stage_w0(experts_of, samples=range(SPG)):
                for s in samples:
                    last = nc.vector.tensor_copy(w0_stage[:, s].rearrange("p k c -> p (k c)"),
                                                 w0_parts[:, bass.ds(experts_of[s], 1)].rearrange("p o k c -> p (o k c)"))
                last.then_inc(w0_staged, len(samples))

            def stage_ob(experts_of):
                for s in range(SPG):
                    last = nc.vector.tensor_copy(ob_stage[0:STACK_ROWS, s, :],
                                                 lora_stack[0:STACK_ROWS, bass.ds(experts_of[s], 1), F:F + D].rearrange("p o c -> p (o c)"))
                last.then_inc(ob_staged, 1)

            def stage_ib(experts_of):
                for s in range(SPG):
                    last = nc.vector.tensor_copy(ib_stage[0:STACK_ROWS, s, :],
                                                 lora_stack[0:STACK_ROWS, bass.ds(experts_of[s], 1), 0:F].rearrange("p o c -> p (o c)"))
                last.then_inc(ib_staged, SPG)

            def stage_factors(experts_of):
                for s in range(SPG):
                    last = nc.vector.tensor_copy(factors_stage[:, s].rearrange("p k r -> p (k r)"),
                                                 factors[:, bass.ds(experts_of[s], 1)].rearrange("p o k r -> p (o k r)"))
                last.then_inc(factors_staged, 1)

            def x_take_rest(q):
                dve.wait_ge(x_high, q + 1)
                nc.vector.tensor_tensor(x_rest[:], halves(turn_bank), x_parts[:, 0], ALU.subtract).then_inc(x_rested, 1)

            def x_add_bias(q):
                b = bias[:, 0:HALVES, bass.ds(SPG * q, SPG)].unsqueeze(3)
                nc.vector.tensor_tensor(x_bias[:].rearrange("p h (s t) -> p h s t", s=SPG),
                                        turn_bank[:, :].rearrange("p (h s t) -> p h s t", h=HALVES, s=SPG),
                                        b.to_broadcast([P, HALVES, SPG, SEQ]), ALU.add).then_inc(x_biased, 1)

            def x_take_low(q):
                dve.wait_ge(x_mid, q + 1)
                nc.vector.tensor_tensor(x_parts[:, 2], x_rest[:], x_parts[:, 1], ALU.subtract).then_inc(x_split, 1)

            def hidden_take_low(g, k):
                dve.wait_ge(hid_high[k], g + 1)
                nc.vector.scalar_tensor_tensor(hid_pair[:, 2 * k:2 * k + 2, 1, :], halves(hidden_banks[k]), 0.0,
                                               hid_pair[:, 2 * k:2 * k + 2, 0, :], ALU.max, ALU.subtract
                                               ).then_inc(hid_split[k], 1)

            def l0_sum(q):
                dve.wait_ge(l0_full, q + 1)
                dve.wait_ge(x_biased, q + 1)
                nc.vector.tensor_tensor(y0[:], halves(front_bank), x_bias[:], ALU.add).then_inc(y0_done, 1)

            def rotate(q):
                dve.wait_ge(rotation_in, 16 * q + 16)
                dve.wait_ge(y0_done, q + 1)
                nc.vector.tensor_tensor(y0_cos[:], y0[:], rotation[:, 0, :].unsqueeze(1).to_broadcast([P, HALVES, GT]),
                                        ALU.mult).then_inc(y0_cos_done, 1)
                nc.vector.tensor_tensor(y0_sin[:], y0[:], rotation[:, 1, :].unsqueeze(1).to_broadcast([P, HALVES, GT]),
                                        ALU.mult).then_inc(y0_sin_done, 1)

            def rotate_sum(q):
                dve.wait_ge(y0_cos_done, q + 1)
                dve.wait_ge(y0_sin_done, q + 1)
                nc.vector.tensor_tensor(y1[:, 0], y0_cos[:, 0], y0_sin[:, 1], ALU.subtract)
                nc.vector.tensor_tensor(y1[:, 1], y0_sin[:, 0], y0_cos[:, 1], ALU.add).then_inc(y1_done, 1)

            def y1_take_rest(q):
                dve.wait_ge(y1_high, q + 1)
                nc.vector.tensor_tensor(y1_rest[:], y1[:], y1_parts[:, 0], ALU.subtract).then_inc(y1_rested, 1)

            def y1_take_low(q):
                dve.wait_ge(y1_mid, q + 1)
                nc.vector.tensor_tensor(y1_parts[:, 2], y1_rest[:], y1_parts[:, 1], ALU.subtract).then_inc(y1_split, 1)

            def low_sum(q, full, summed):
                dve.wait_ge(full, q + 1)
                products = low_bank[0:2 * RANK, :].rearrange("p (s a t) -> p s t a", s=SPG, a=2)
                nc.vector.tensor_reduce(low[:].rearrange("p (s t) -> p s t", s=SPG), products,
                                        mybir.AxisListType.X, ALU.add).then_inc(summed, 1)

            def low_take_low(q, high, split):
                dve.wait_ge(high, q + 1)
                nc.vector.tensor_tensor(low_pair[2 * RANK:4 * RANK], low[:], low_pair[0:2 * RANK], ALU.subtract
                                        ).then_inc(split, 1)

            def stack_take_rest(q, high, rested):
                dve.wait_ge(high, q + 1)
                nc.vector.tensor_tensor(stack_rest[0:STACK_MIDS], stack_bank[0:STACK_MIDS],
                                        stack[0:STACK_MIDS], ALU.subtract).then_inc(rested, 1)

            def stack_take_low(q, mid, done):
                dve.wait_ge(mid, q + 1)
                nc.vector.tensor_tensor(stack[0:STACK_LOWS], stack_rest[0:STACK_LOWS],
                                        stack[0:STACK_LOWS], ALU.subtract).then_inc(done, 1)

            def l2_sum(q):
                dve.wait_ge(l2_full, q + 1)
                dve.wait_ge(y1_biased, q + 1)
                nc.vector.tensor_tensor(y2[:, bass.ds(q % 2, 1)].rearrange("p o h t -> p (o h) t"),
                                        halves(front_bank), y1_bias[:], ALU.add).then_inc(y2_done, 1)

            def y2_take_low(q):
                dve.wait_ge(y2_high, q + 1)
                nc.vector.tensor_tensor(y2_pair[:, :, 1], y2[:, bass.ds(q % 2, 1)].rearrange("p o h t -> p (o h) t"),
                                        y2_pair[:, :, 0], ALU.subtract).then_inc(y2_split, 1)

            def l3_sum(g):
                dve.wait_ge(out_full, g + 1)
                nc.vector.tensor_tensor(y3[:], halves(out_bank),
                                        y2[:, bass.ds(g % 2, 1)].rearrange("p o h t -> p (o h) t"),
                                        ALU.add).then_inc(y3_done, 1)

            def body(g, middle, front):
                n, m = g + 1, g + 2
                if front:
                    next_experts_of = group_indices(VECTOR, 0, m)
                    stage_w0(next_experts_of, [0, 1])
                    x_take_rest(m)
                hidden_take_low(g, 0)
                hidden_take_low(g, 1)
                hidden_take_low(g, 2)
                hidden_take_low(g, 3)
                if front:
                    x_add_bias(m)
                    x_take_low(m)
                if middle:
                    experts_of = group_indices(VECTOR, 0, n)
                    l2_sum(n)
                if front:
                    stage_w0(next_experts_of, [2, 3])
                if middle:
                    y2_take_low(n)
                low_sum(g, low2_full, low2_summed)
                low_take_low(g, low2_high, low2_split)
                if middle:
                    stage_factors(experts_of)
                stack_take_rest(g, stack2_high, stack2_rested)
                stack_take_low(g, stack2_mid, stack2_done)
                if front:
                    l0_sum(m)
                    rotate(m)
                    rotate_sum(m)
                if middle:
                    low_sum(n, low1_full, low1_summed)
                l3_sum(g)
                if middle:
                    low_take_low(n, low1_high, low1_split)
                if front:
                    y1_take_rest(m)
                if middle:
                    stack_take_rest(n, stack1_high, stack1_rested)
                    stage_ob(experts_of)
                    stack_take_low(n, stack1_mid, stack1_done)
                if front:
                    y1_take_low(m)

            experts_of = group_indices(VECTOR, 0, 0)
            dve.wait_ge(pre_full, EARLY)
            x_take_rest(0)
            dve.wait_ge(pre_high, EARLY)
            dve.wait_ge(pre_mid, len(THREES))
            dve.wait_ge(pre_low, len(THREES))
            stage_w0(experts_of)
            x_take_low(0)
            x_add_bias(0)
            take_jobs(EARLY, EARLY + 4)
            l0_sum(0)
            rotate(0)
            rotate_sum(0)
            x_take_rest(1)
            y1_take_rest(0)
            x_add_bias(1)
            y1_take_low(0)
            x_take_low(1)
            stage_w0(group_indices(VECTOR, 0, 1))
            take_jobs(EARLY + 4, len(JOBS))
            dve.wait_ge(pre_high, len(JOBS))
            dve.wait_ge(pre_rest, RESTS[-1])
            l2_sum(0)
            stage_factors(experts_of)
            y2_take_low(0)
            dve.wait_ge(pre_full, len(JOBS))
            dve.wait_ge(rot_saved, 32)
            dve.wait_ge(parts_saved, 16)
            dve.wait_ge(spread_ready, 1)
            dve.wait_ge(in_stack, 16 * len(STACK_ROW))
            stage_ib(experts_of)
            l0_sum(1)
            low_sum(0, low1_full, low1_summed)
            low_take_low(0, low1_high, low1_split)
            rotate(1)
            rotate_sum(1)
            stack_take_rest(0, stack1_high, stack1_rested)
            stage_ob(experts_of)
            stack_take_low(0, stack1_mid, stack1_done)
            y1_take_rest(1)
            y1_take_low(1)
            with dve.Fori(0, GROUPS - 2) as g:
                body(g, True, True)
            body(GROUPS - 2, True, False)
            body(GROUPS - 1, False, False)

        @block.tensor
        def _(pe):
            pe.wait_ge(in_ident, 16)

            def free(j):
                before = [i for i in range(j) if JOB_BANK[i] == JOB_BANK[j]]
                if before:
                    pe.wait_ge(pre_high, before[-1] + 1)
                    pe.wait_ge(pre_rest, RESTS[before[-1]])

            def turn_x(q):
                pe.wait_ge(x_in, 16 * q + 16)
                for t in range(TILES):
                    for h in range(HALVES):
                        last = nc.tensor.transpose(halves(turn_bank)[:, h, P * t:P * (t + 1)],
                                                   x_sb[:, t, P * h:P * (h + 1)], ident[:])
                last.then_inc(x_turned, 1)

            arrived = {
                "ia": (in_ia, 16), "oa": (in_oa, 16), "ib": (in_lora_b, 16 * (FT + HALVES)), "cib": (in_common, 64),
                "wo": (in_wo, 16), "bias": (in_bias, 64),
            }

            def fill_banks(first, last):
                for j in range(first, last):
                    how, name, n = JOBS[j]
                    bank = banks[JOB_BANK[j]]
                    free(j)
                    if name in arrived and n == 0:
                        pe.wait_ge(*arrived[name])
                    if name == "w0":
                        pe.wait_ge(in_w0[n], 16)
                        for k in range(HALVES):
                            for h in range(HALVES):
                                last = nc.tensor.transpose(bank[:, D * k + P * h:D * k + P * (h + 1)],
                                                           w0_nat[:, n, h, P * k:P * (k + 1)], ident[:])
                    if name == "ia":
                        for h in range(HALVES):
                            last = nc.tensor.transpose(bank[:, P * h:P * (h + 1)], ia_nat[:, P * h:P * (h + 1)], ident[:])
                    if name == "oa":
                        for i in range(4):
                            t = 4 * n + i
                            last = nc.tensor.transpose(bank[:, P * i:P * (i + 1)], oa_nat[:, P * t:P * (t + 1)], ident[:])
                    if name == "ib":
                        for i in range(4):
                            last = nc.tensor.transpose(bank[:, P * i:P * (i + 1)], ib_nat[:, 4 * n + i, :], ident[:])
                    if name == "ob":
                        for h in range(HALVES):
                            last = nc.tensor.transpose(bank[:, P * h:P * (h + 1)], ob_nat[:, h, :], ident[:])
                    if name == "cib":
                        for i in range(4):
                            last = nc.tensor.transpose(bank[0:RANK, P * i:P * (i + 1)], cib_nat[:, 4 * n + i, :], ident[:])
                    if name == "cob":
                        for h in range(HALVES):
                            last = nc.tensor.transpose(bank[0:RANK, P * h:P * (h + 1)], cob_nat[:, h, :], ident[:])
                    if name == "bias":
                        pe.wait_ge(hot_done, 1)
                        for layer, (table, rows) in enumerate(((b0_nat, EXPERTS), (b2_nat, CATEGORIES))):
                            for h in range(HALVES):
                                c = BATCH * (HALVES * layer + h)
                                last = nc.tensor.matmul(bank[:, c:c + BATCH], table[0:rows, P * h:P * (h + 1)],
                                                        one_hot[0:rows, layer, :], start=True, stop=True)
                    if name == "wi":
                        k, half = n % 2, n // 2
                        pe.wait_ge(in_wi[half], 16)
                        if n == 0:
                            pe.wait_ge(cia_scaled, 1)
                            pe.wait_ge(pre_high, job("cob") + 1)
                        nc.tensor.matmul(bank[:, :], cia2[:, P * k:P * (k + 1)], cib_t[:, 512 * half:512 * half + 512],
                                         start=True, stop=True, skip_group_check=True)
                        for i in range(4):
                            last = nc.tensor.matmul(bank[:, P * i:P * (i + 1)], wi_nat[:, 4 * half + i, P * k:P * (k + 1)],
                                                    ident[:], start=False, stop=True, skip_group_check=True)
                    if name == "wo":
                        if n == 0:
                            pe.wait_ge(coa_scaled, 1)
                        for i in range(2):
                            t = 2 * n + i
                            nc.tensor.matmul(bank[:, D * i:D * (i + 1)], coa2[:, P * t:P * (t + 1)], cob_t[:],
                                             start=True, stop=True, skip_group_check=True)
                            for h in range(HALVES):
                                last = nc.tensor.matmul(bank[:, D * i + P * h:D * i + P * (h + 1)],
                                                        wo_nat[:, h, P * t:P * (t + 1)], ident[:],
                                                        start=False, stop=True, skip_group_check=True)
                    last.then_inc(pre_full, 1)

            fill_banks(0, EARLY - 1)
            last_there = max(i for i in range(EARLY) if JOB_BANK[i] == 0)
            pe.wait_ge(pre_high, last_there + 1)
            pe.wait_ge(pre_rest, RESTS[last_there])
            turn_x(0)
            fill_banks(EARLY - 1, EARLY)

            def per_sample(weights, parts, full):
                for h in range(HALVES):
                    for s in range(SPG):
                        count = 0
                        for w_part, a_part in PRODUCTS:
                            for k in range(HALVES):
                                c = D * k + P * h
                                last = nc.tensor.matmul(halves(front_bank)[:, h, SEQ * s:SEQ * (s + 1)],
                                                        weights[:, s, w_part, c:c + P],
                                                        parts[:, a_part, k, SEQ * s:SEQ * (s + 1)],
                                                        start=(count == 0), stop=(count == 2 * len(PRODUCTS) - 1))
                                count += 1
                last.then_inc(full, 1)

            def l0(q):
                pe.wait_ge(x_split, q + 1)
                pe.wait_ge(w0_staged, SPG * q + SPG)
                per_sample(w0_stage, x_parts, l0_full)

            def l2(q):
                pe.wait_ge(y1_split, q + 1)
                for s in range(SPG):
                    pe.wait_ge(w2_split[s], q + 1)
                per_sample(w2_parts, y1_parts, l2_full)

            def three(bank, w_hi, w_lo, a_hi, a_lo, start=False, stop=False):
                nc.tensor.matmul(bank, w_lo, a_hi, start=start, stop=False, skip_group_check=True)
                nc.tensor.matmul(bank, w_hi, a_lo, start=False, stop=False, skip_group_check=True)
                return nc.tensor.matmul(bank, w_hi, a_hi, start=False, stop=stop, skip_group_check=True)

            def low_products(q_tiles, first, pair):
                for s in range(SPG):
                    for k in range(q_tiles):
                        last = nc.tensor.matmul(low_bank[0:2 * RANK, 2 * SEQ * s:2 * SEQ * (s + 1)],
                                                factors_stage[:, s, first + k, :],
                                                pair[:, k, :, SEQ * s:SEQ * (s + 1)],
                                                start=(k == 0), stop=(k == q_tiles - 1))
                return last

            def low1(q):
                pe.wait_ge(y2_split, q + 1)
                pe.wait_ge(factors_staged, q + 1)
                low_products(HALVES, FT, y2_pair).then_inc(low1_full, 1)

            def low2(g):
                for k in range(PAIRS):
                    pe.wait_ge(hid_split[k], g + 1)
                low_products(FT, 0, hid_pair).then_inc(low2_full, 1)

            def spread_low(q, split, full):
                pe.wait_ge(split, q + 1)
                nc.tensor.matmul(stack_bank, spread_sb[:], low_pair[:], start=True, stop=True).then_inc(full, 1)

            def hidden_base(k):
                for i in range(2):
                    f = 2 * k + i
                    for h in range(HALVES):
                        three(halves(hidden_banks[k])[:, i, :], wi_hi[:, h, P * f:P * (f + 1)],
                              wi_lo[:, h, P * f:P * (f + 1)], y2_pair[:, h, 0, :], y2_pair[:, h, 1, :],
                              start=(i == 0 and h == 0), stop=(h == HALVES - 1))

            def hidden_lora(k):
                for i in range(2):
                    f = 2 * k + i
                    for s in range(SPG):
                        last = nc.tensor.matmul(halves(hidden_banks[k])[:, i, SEQ * s:SEQ * (s + 1)],
                                                ib_stage[0:STACK_ROWS, s, P * f:P * (f + 1)],
                                                stack[0:STACK_ROWS, SEQ * s:SEQ * (s + 1)],
                                                start=False, stop=True, skip_group_check=True)
                last.then_inc(hidden_full[k], 1)

            def out_half(h, waiting_for=None):
                for k in range(FT):
                    if waiting_for is not None and k % 2 == 0:
                        pe.wait_ge(hid_split[k // 2], waiting_for + 1)
                    three(halves(out_bank)[:, h, :], wo_hi[:, k, P * h:P * (h + 1)], wo_lo[:, k, P * h:P * (h + 1)],
                          hid_pair[:, k, 0, :], hid_pair[:, k, 1, :], start=(h == 0 and k == 0), stop=(k == FT - 1))

            def out_lora(g):
                pe.wait_ge(stack2_done, g + 1)
                pe.wait_ge(ob_staged, g + 1)
                for h in range(HALVES):
                    for s in range(SPG):
                        last = nc.tensor.matmul(halves(out_bank)[:, h, SEQ * s:SEQ * (s + 1)],
                                                ob_stage[0:STACK_ROWS, s, P * h:P * (h + 1)],
                                                stack[0:STACK_ROWS, SEQ * s:SEQ * (s + 1)],
                                                start=False, stop=True, skip_group_check=True)
                last.then_inc(out_full, 1)

            def turn_out(g, q):
                pe.wait_ge(y3_done, g + 1)
                pe.wait_ge(x_biased, q + 1)
                for t in range(TILES):
                    for h in range(HALVES):
                        last = nc.tensor.transpose(turn_bank[:, D * t + P * h:D * t + P * (h + 1)],
                                                   y3[:, h, P * t:P * (t + 1)], ident[:])
                last.then_inc(out_turned, 1)

            def body(g, middle, front):
                n, m = g + 1, g + 2
                hidden_base(2)
                if front:
                    pe.wait_ge(out_taken, g + 1)
                    turn_x(m)
                pe.wait_ge(stack1_done, g + 1)
                pe.wait_ge(ib_staged, SPG * g + SPG)
                hidden_lora(0)
                hidden_lora(1)
                hidden_base(3)
                hidden_lora(2)
                hidden_lora(3)
                if middle:
                    l2(n)
                    low2(g)
                    out_half(0)
                else:
                    out_half(0, waiting_for=g)
                    low2(g)
                    out_half(1)
                spread_low(g, low2_split, spread2_full)
                if front:
                    pe.wait_ge(y2_done, n + 1)
                    l0(m)
                if middle:
                    out_half(1)
                    pe.wait_ge(stack2_rested, g + 1)
                    low1(n)
                out_lora(g)
                if middle:
                    hidden_base(0)
                turn_out(g, m if front else GROUPS - 1)
                if middle:
                    spread_low(n, low1_split, spread1_full)
                    hidden_base(1)

            fill_banks(EARLY, EARLY + 4)
            l0(0)
            pe.wait_ge(x_biased, 1)
            turn_x(1)
            fill_banks(EARLY + 4, len(JOBS))
            l2(0)
            pe.wait_ge(y2_done, 1)
            l0(1)
            low1(0)
            hidden_base(0)
            pe.wait_ge(spread_ready, 1)
            spread_low(0, low1_split, spread1_full)
            hidden_base(1)
            with pe.Fori(0, GROUPS - 2) as g:
                body(g, True, True)
            body(GROUPS - 2, True, False)
            body(GROUPS - 1, False, False)


_INS = ['x', 'itok_B_0_7', 'condB_deltat', 'itok_B_0_63', 'L0_cond_weight', 'L0_cond_bias',
        'L1_cond_amplitudes', 'L1_cond_frequencies', 'L2_cond_W', 'L2_cond_b', 'L3_cond_wi', 'L3_cond_wo',
        'L3_cond_common_wi_a', 'L3_cond_common_wi_b', 'L3_cond_common_wo_a', 'L3_cond_common_wo_b',
        'L3_cond_experts_wi_a', 'L3_cond_experts_wi_b', 'L3_cond_experts_wo_a', 'L3_cond_experts_wo_b']
_OUT = ((BATCH, SEQ, D), 'float32')


def kernel(**inputs):
    import concourse.bacc as _bacc
    from concourse.bass_utils import run_bass_kernel_spmd as _run

    nc = _bacc.Bacc("TRN2", target_bir_lowering=False, num_devices=1)
    arrays, args = {}, []
    given = {name: np.ascontiguousarray(inputs[name]) for name in _INS}
    given["identity"] = np.eye(P, dtype=np.float32)
    given["spread"] = spread_constants()
    given["numbers"] = number_constants()
    for name, a in given.items():
        arrays[f"in_{name}_dram"] = a
        args.append(nc.dram_tensor(f"in_{name}_dram", a.shape, mybir.dt.from_np(a.dtype), kind="ExternalInput").ap())
    args.append(nc.dram_tensor("out_0_dram", _OUT[0], FP32, kind="ExternalOutput").ap())
    cond_resid_kernel(nc, *args)
    r = _run(nc, [arrays], core_ids=[0])
    return r.results[0]["out_0_dram"]
```
